# Optimizing a Trainium2 kernel written in Bass

```python
import numpy as np
import jax
import jax.numpy as jnp

def _softmax(x, axis=-1):
    return jax.nn.softmax(x, axis=axis)

def _gelu(x):
    return jax.nn.gelu(x, approximate=True)

def _silu(x):
    return jax.nn.silu(x)

def _sigmoid(x):
    return jax.nn.sigmoid(x)

def _layernorm(x, axis=-1, eps=1e-05):
    m = jnp.mean(x, axis=axis, keepdims=True)
    v = jnp.var(x, axis=axis, keepdims=True)
    return (x - m) / jnp.sqrt(v + eps)

def _scatter_add(tgt, idx, src, axis=0):
    return tgt.at[idx].add(src)

def _segment_sum(src, seg, n):
    return jax.ops.segment_sum(src, seg, n)
kernel_name = 'mk_hybrid_d1_jaxref_r8_fe28d7'

def setup_inputs(seed: int=0):
    np.random.seed(seed)
    _w = jnp.asarray

    def _L0_attn_a_setup():
        import jax, jax.numpy as jnp
        import numpy as np
        D_MODEL, N_HEADS, N_KV, HEAD_DIM, D_LAT = (128, 8, 2, 128, 32)
        N_REP = N_HEADS // N_KV
        B, T = (2, 256)
        key = jax.random.key(seed)
        ks = jax.random.split(key, 8)
        s = lambda fan_in: 1.0 / np.sqrt(fan_in)
        return {'x': jax.random.normal(ks[0], (B, T, D_MODEL), jnp.float32), 'wq': jax.random.normal(ks[1], (D_MODEL, N_HEADS * HEAD_DIM), jnp.float32) * s(D_MODEL), 'wk_down': jax.random.normal(ks[2], (D_MODEL, N_KV * D_LAT), jnp.float32) * s(D_MODEL), 'wv_down': jax.random.normal(ks[3], (D_MODEL, N_KV * D_LAT), jnp.float32) * s(D_MODEL), 'wk_up': jax.random.normal(ks[4], (D_LAT, HEAD_DIM), jnp.float32) * s(D_LAT), 'wv_up': jax.random.normal(ks[5], (D_LAT, HEAD_DIM), jnp.float32) * s(D_LAT), 'wo': jax.random.normal(ks[6], (N_HEADS * HEAD_DIM, D_MODEL), jnp.float32) * s(N_HEADS * HEAD_DIM)}
    _L0_attn_a_in = _L0_attn_a_setup()

    def _L0_attn_b_setup():
        import jax, jax.numpy as jnp
        import numpy as np
        HEAD_DIM = 64
        ROPE_BASE = 10000.0

        def _rope(y):
            B, H, T, hd = y.shape
            theta = jnp.exp(jnp.log(ROPE_BASE) * jnp.arange(hd // 2, dtype=jnp.float32) / hd)
            args = jnp.arange(T, dtype=jnp.float32)[:, None] * theta
            c, s = (jnp.cos(args), jnp.sin(args))
            y2 = y.reshape(B, H, T, hd // 2, 2)
            x0, x1 = (y2[..., 0], y2[..., 1])
            return jnp.stack([x0 * c - x1 * s, x0 * s + x1 * c], axis=-1).reshape(B, H, T, hd)
        key = jax.random.key(seed)
        ks = jax.random.split(key, 5)
        B, T, D = (2, 256, 128)
        scale = 1.0 / np.sqrt(D)
        return {'x': jax.random.normal(ks[0], (B, T, D), dtype=jnp.float32), 'wq': jax.random.normal(ks[1], (D, D), dtype=jnp.float32) * scale, 'wk': jax.random.normal(ks[2], (D, D), dtype=jnp.float32) * scale, 'wv': jax.random.normal(ks[3], (D, D), dtype=jnp.float32) * scale, 'wo': jax.random.normal(ks[4], (D, D), dtype=jnp.float32) * scale}
    _L0_attn_b_in = _L0_attn_b_setup()

    def _L0_ffn_setup():
        import jax, jax.numpy as jnp
        import numpy as np
        B, L, D, E, K, DFF = (2, 256, 128, 8, 2, 512)
        key = jax.random.key(seed)
        kx, kr, kg, ku, kd = jax.random.split(key, 5)
        scale = 0.02
        return {'x': jax.random.normal(kx, (B, L, D), dtype=jnp.float32), 'Wr': jax.random.normal(kr, (E, D), dtype=jnp.float32) * scale, 'Wg': jax.random.normal(kg, (E, DFF, D), dtype=jnp.float32) * scale, 'Wu': jax.random.normal(ku, (E, DFF, D), dtype=jnp.float32) * scale, 'Wd': jax.random.normal(kd, (E, D, DFF), dtype=jnp.float32) * scale}
    _L0_ffn_in = _L0_ffn_setup()
    _d = {'L0_attn_a_x': _L0_attn_a_in['x'], 'L0_attn_a_wq': _L0_attn_a_in['wq'], 'L0_attn_a_wk_down': _L0_attn_a_in['wk_down'], 'L0_attn_a_wv_down': _L0_attn_a_in['wv_down'], 'L0_attn_a_wk_up': _L0_attn_a_in['wk_up'], 'L0_attn_a_wv_up': _L0_attn_a_in['wv_up'], 'L0_attn_a_wo': _L0_attn_a_in['wo'], 'L0_attn_b_wq': _L0_attn_b_in['wq'], 'L0_attn_b_wk': _L0_attn_b_in['wk'], 'L0_attn_b_wv': _L0_attn_b_in['wv'], 'L0_attn_b_wo': _L0_attn_b_in['wo'], 'L0_ffn_Wr': _L0_ffn_in['Wr'], 'L0_ffn_Wg': _L0_ffn_in['Wg'], 'L0_ffn_Wu': _L0_ffn_in['Wu'], 'L0_ffn_Wd': _L0_ffn_in['Wd']}
    _x0 = _d['L0_attn_a_x']
    _d['L0_attn_a_x'] = jax.random.normal(jax.random.fold_in(jax.random.key(seed), 1), (8, 512, 128), dtype=_x0.dtype)
    del _x0
    return _d

def reference(L0_attn_a_x, L0_attn_a_wq, L0_attn_a_wk_down, L0_attn_a_wv_down, L0_attn_a_wk_up, L0_attn_a_wv_up, L0_attn_a_wo, L0_attn_b_wq, L0_attn_b_wk, L0_attn_b_wv, L0_attn_b_wo, L0_ffn_Wr, L0_ffn_Wg, L0_ffn_Wu, L0_ffn_Wd):

    def _L0_attn_a_ref(x, wq, wk_down, wv_down, wk_up, wv_up, wo):
        import jax, jax.numpy as jnp
        import numpy as np
        D_MODEL, N_HEADS, N_KV, HEAD_DIM, D_LAT = (128, 8, 2, 128, 32)
        N_REP = N_HEADS // N_KV
        B, T = (2, 256)
        Bq, Tq, _ = x.shape
        scale = HEAD_DIM ** (-0.5)
        q = (x @ wq).reshape(Bq, Tq, N_KV, N_REP, HEAD_DIM)
        k_lat = (x @ wk_down).reshape(Bq, Tq, N_KV, D_LAT)
        v_lat = (x @ wv_down).reshape(Bq, Tq, N_KV, D_LAT)
        k = jnp.einsum('bkhl,ld->bkhd', k_lat, wk_up)
        v = jnp.einsum('bkhl,ld->bkhd', v_lat, wv_up)
        scores = jnp.einsum('bqhrd,bkhd->bhrqk', q, k) * scale
        causal = jnp.tril(jnp.ones((Tq, Tq), dtype=bool))
        scores = jnp.where(causal, scores, jnp.finfo(scores.dtype).min)
        probs = jax.nn.softmax(scores, axis=-1)
        y = jnp.einsum('bhrqk,bkhd->bqhrd', probs, v)
        y = y.reshape(Bq, Tq, N_HEADS * HEAD_DIM)
        return y @ wo

    def _L0_attn_b_ref(x, wq, wk, wv, wo):
        import jax, jax.numpy as jnp
        import numpy as np
        HEAD_DIM = 64
        ROPE_BASE = 10000.0

        def _rope(y):
            B, H, T, hd = y.shape
            theta = jnp.exp(jnp.log(ROPE_BASE) * jnp.arange(hd // 2, dtype=jnp.float32) / hd)
            args = jnp.arange(T, dtype=jnp.float32)[:, None] * theta
            c, s = (jnp.cos(args), jnp.sin(args))
            y2 = y.reshape(B, H, T, hd // 2, 2)
            x0, x1 = (y2[..., 0], y2[..., 1])
            return jnp.stack([x0 * c - x1 * s, x0 * s + x1 * c], axis=-1).reshape(B, H, T, hd)
        B, T, D = x.shape
        hd = HEAD_DIM
        H = D // hd
        qk_scale = hd ** (-0.25)

        def split_heads(y):
            return y.reshape(B, T, H, hd).transpose(0, 2, 1, 3)
        q = split_heads(x @ wq.T) * qk_scale
        k = split_heads(x @ wk.T) * qk_scale
        v = split_heads(x @ wv.T)
        q, k = (_rope(q), _rope(k))
        mask = jnp.where(jnp.tril(jnp.ones((T, T), dtype=bool)), 0.0, -jnp.inf).astype(x.dtype)
        energy = jnp.einsum('bhtd,bhld->bhtl', q, k) + mask
        attn = jax.nn.softmax(energy, axis=-1)
        out = jnp.einsum('bhtl,bhld->bhtd', attn, v)
        out = out.transpose(0, 2, 1, 3).reshape(B, T, D)
        return out @ wo.T

    def _L0_ffn_ref(x, Wr, Wg, Wu, Wd):
        import jax, jax.numpy as jnp
        import numpy as np
        B, L, D, E, K, DFF = (2, 256, 128, 8, 2, 512)
        Bb, Ll, Dd = x.shape
        T = Bb * Ll
        xt = x.reshape(T, Dd)
        logits = jnp.einsum('td,ed->te', xt, Wr)
        scores = jax.nn.softmax(logits, axis=-1)
        k_scores, k_ids = jax.lax.top_k(scores, K)
        eps = jnp.finfo(x.dtype).eps
        k_w = k_scores / (k_scores.sum(axis=-1, keepdims=True) + eps)
        combine = jnp.sum(jax.nn.one_hot(k_ids, E, dtype=x.dtype) * k_w[..., None], axis=1)
        g = jnp.einsum('td,efd->etf', xt, Wg)
        u = jnp.einsum('td,efd->etf', xt, Wu)
        h = jax.nn.relu(g) * u
        out_e = jnp.einsum('etf,edf->etd', h, Wd)
        out = jnp.einsum('te,etd->td', combine, out_e)
        return out.reshape(Bb, Ll, Dd)
    x = L0_attn_a_x
    x = x + _L0_attn_a_ref(_layernorm(x, axis=-1), L0_attn_a_wq, L0_attn_a_wk_down, L0_attn_a_wv_down, L0_attn_a_wk_up, L0_attn_a_wv_up, L0_attn_a_wo)
    x = x + _L0_ffn_ref(_layernorm(x, axis=-1), L0_ffn_Wr, L0_ffn_Wg, L0_ffn_Wu, L0_ffn_Wd)
    x = x + _L0_attn_b_ref(_layernorm(x, axis=-1), L0_attn_b_wq, L0_attn_b_wk, L0_attn_b_wv, L0_attn_b_wo)
    x = x + _L0_ffn_ref(_layernorm(x, axis=-1), L0_ffn_Wr, L0_ffn_Wg, L0_ffn_Wu, L0_ffn_Wd)
    return x

_drawn_inputs = setup_inputs


def setup_inputs(seed=0):
    import zlib

    import numpy as np

    out = dict(_drawn_inputs(seed))
    spreads = {}
    factors = {'L0_ffn_Wr': 2.996, 'L0_ffn_Wg': 3.113}
    for name, (base, spread) in spreads.items():
        noise = np.random.default_rng([zlib.crc32(name.encode()), seed]).standard_normal(out[name].shape)
        drawn = base * np.exp(spread * noise) if base else spread * noise
        out[name] = jnp.asarray(drawn.astype(out[name].dtype))
    for name, factor in factors.items():
        out[name] = (out[name] * factor).astype(out[name].dtype)
    return out
```

```python
from contextlib import ExitStack

import numpy as np

import concourse.bass as bass
from concourse import mybir

ALU = mybir.AluOpType
ACT = mybir.ActivationFunctionType
AX_X = mybir.AxisListType.X
F32 = mybir.dt.float32
F32R = mybir.dt.float32r
BF16 = mybir.dt.bfloat16
I32 = mybir.dt.int32
U32 = mybir.dt.uint32

P = 128
BATCH = 8
SEQ = 512
D = 128
TPB = SEQ // P
NT = BATCH * TPB
TOKENS = NT * P
LN_EPS = 1e-5
RSQRT_MAGIC = 0x5F3759DF

HA, GA, DA, HDA = 8, 2, 32, 128
HB, DB = 2, 64
ROPE_BASE = 10000.0

E, FF = 8, 512
FC = FF // P
REGION = TOKENS + P
DUMMY_ROW = E * REGION
ROWS = DUMMY_ROW + P
XROW = D + 1
STEPS = 2 * TOKENS // P + E
NOWHERE = 1 << 20
TOPK_EPS = float(np.finfo(np.float32).eps)
MASKED = -1e30

S_PLACE = [(1, 384), (2, 0), (1, 0), (0, 0)]
ST_PLACE = [(0, 0), (1, 0), (2, 0), (1, 384)]
P_START = [0, 512, 1024, 896]
BANK_COLS = [512, 512, 256]


def make_constants():
    c = {}
    c["ident"] = np.eye(P, dtype=np.float32)
    q, k = np.arange(P)[:, None], np.arange(P)[None, :]
    c["causal"] = np.where(k > q, np.float32(MASKED), np.float32(0)).astype(np.float32)
    c["before"] = (q < k).astype(np.float32)
    sel = np.zeros((HA, HA, P), np.float32)
    for h in range(HA):
        sel[h, h] = 1
    c["select"] = sel
    theta = np.exp((np.log(np.float32(ROPE_BASE)) * np.arange(DB // 2, dtype=np.float32)
                    / np.float32(DB)).astype(np.float64)).astype(np.float32)
    args = (theta[:, None] * np.arange(SEQ, dtype=np.float32)[None, :]).astype(np.float64)
    scale = DB ** -0.25
    c["rope_cos"] = np.tile(np.cos(args) * scale, (2 * HB, 1)).astype(np.float32)
    sin = np.sin(args) * scale
    c["rope_sin"] = np.tile(np.concatenate([-sin, sin]), (HB, 1)).astype(np.float32)
    c["rank_rev"] = np.tile(np.repeat(np.arange(E, 0, -1, dtype=np.float32), NT), (P, 1))
    c["region"] = np.tile(np.repeat(np.arange(E, dtype=np.float32) * REGION, NT), (P, 1))
    carry = np.ones((E, NT), np.float32)
    carry[:, 0] = 0
    c["carry"] = np.tile(carry.reshape(1, -1), (P, 1))
    c["step_no"] = np.repeat(np.arange(STEPS, dtype=np.float32), E)[None, :]
    c["expert_row"] = (np.arange(E, dtype=np.float32) * REGION)[None, :]
    t, p = np.arange(NT)[None, None, :], np.arange(P)[:, None, None]
    c["dest"] = (np.arange(2)[None, :, None] * TOKENS + t * P + p).astype(np.uint32).view(np.int32)
    pad = np.zeros((P, XROW), np.float32)
    pad[:, D] = np.full(P, NOWHERE, np.uint32).view(np.float32)
    c["pad"] = pad
    return c


CONST_NAMES = ["ident", "causal", "before", "select", "rope_cos", "rope_sin", "rank_rev", "region",
               "carry", "step_no", "expert_row", "dest", "pad"]


def flat(ap):
    return ap.rearrange("p a n -> p (a n)")


def build(nc, io, stages=4):
    ctx = ExitStack()

    def sb(name, shape, dt=F32, on=ctx):
        return on.enter_context(nc.sbuf_tensor("sb_" + name, shape, dt))

    def psum(name, on):
        return on.enter_context(nc.psum_tensor("ps_" + name, [P, 512], F32))

    def sem(name):
        return ctx.enter_context(nc.semaphore(name))

    def chain(eng, s, base=0):
        n = [0]

        def link(ins):
            n[0] += 1
            ins.then_inc(s, 1)
            eng.wait_ge(s, base + n[0])
        link.count = n
        return link

    with ctx:
        x = sb("x", [P, NT, D])
        w_hi = sb("w_hi", [P, E * 3 * FF], F32R)
        w_lo = sb("w_lo", [P, E * 3 * FF], F32R)
        ident = sb("ident", [P, P])
        causal = sb("causal", [P, P])
        ident_b = sb("ident_b", [P, P], BF16)
        causal_b = sb("causal_b", [P, P], BF16)
        mean = sb("mean", [P, NT])
        rstd = sb("rstd", [P, NT])
        weight = sb("weight", [P, 2, NT])

        gathered = nc.dram_tensor("gathered", (ROWS, XROW), F32, kind="Internal").ap()
        by_token = nc.dram_tensor("by_token", (2 * TOKENS, D), F32, kind="Internal").ap()

        def setup():
            on = ExitStack()
            with on:
                raw = sb("w_raw", [P, 2, 3 * FF], on=on)
                loaded, w_loaded = sem("loaded"), [sem("w_loaded0"), sem("w_loaded1")]
                hi_done, lo_done, conv = sem("w_hi_done"), sem("w_lo_done"), sem("conv")
                with nc.Block() as block:
                    @block.sync
                    def _(sp):
                        sp.dma_start(ident[:], io["ident"]).then_inc(loaded, 16)
                        sp.dma_start(causal[:], io["causal"]).then_inc(loaded, 16)
                        sp.dma_start(x[:], io["x"].rearrange("b (t p) d -> p (b t) d", p=P)).then_inc(loaded, 16)
                        for e in range(E):
                            if e >= 2:
                                sp.wait_ge(lo_done, e - 1)
                            sp.dma_start(raw[:, e % 2, :], io["w_ffn"][:, e, :]).then_inc(w_loaded[e % 2], 16)

                    @block.scalar
                    def _(act):
                        for e in range(E):
                            act.wait_ge(w_loaded[e % 2], 16 * (e // 2 + 1))
                            act.copy(w_hi[:, bass.ts(e, 3 * FF)], raw[:, e % 2, :]).then_inc(hi_done, 1)

                    @block.vector
                    def _(dve):
                        dve.wait_ge(loaded, 48)
                        dve.tensor_copy(ident_b[:], ident[:]).then_inc(conv, 1)
                        dve.tensor_copy(causal_b[:], causal[:]).then_inc(conv, 1)
                        for e in range(E):
                            dve.wait_ge(hi_done, e + 1)
                            w = bass.ts(e, 3 * FF)
                            dve.tensor_tensor(w_lo[:, w], raw[:, e % 2, :], w_hi[:, w].bitcast(F32),
                                              ALU.subtract).then_inc(lo_done, 1)

        def norm_scratch(on, tag):
            return dict(st=sb(f"stats_{tag}", [P, NT, 6], on=on), t=sb(f"ln_t_{tag}", [P, 4, NT], on=on),
                        i=sb(f"ln_i_{tag}", [P, 2, NT], I32, on=on))

        def norm_stats(dve, s, step):
            st, t, i = s["st"], s["t"], s["i"]
            for n in range(NT):
                ins = dve.bn_stats(st[:, n, :], x[:, n, :])
            step(ins)
            v, d, y, u = (t[:, k, :] for k in range(4))
            step(dve.tensor_tensor(mean[:], st[:, :, 1], st[:, :, 4], ALU.add))
            step(dve.tensor_tensor(d, st[:, :, 1], st[:, :, 4], ALU.subtract))
            step(dve.tensor_tensor(v, st[:, :, 2], st[:, :, 5], ALU.add))
            step(dve.tensor_scalar(mean[:], mean[:], 0.5, None, ALU.mult))
            step(dve.tensor_scalar(v, v, 1.0 / D, LN_EPS, ALU.mult, ALU.add))
            step(dve.scalar_tensor_tensor(out=u, in0=d, scalar=0.25, in1=d, op0=ALU.mult, op1=ALU.mult))
            step(dve.tensor_tensor(v, v, u, ALU.add))
            step(dve.tensor_scalar(i[:, 0, :], v.bitcast(I32), 1, None, ALU.logical_shift_right))
            step(dve.tensor_scalar(i[:, 1, :], i[:, 0, :], -1.0, float(RSQRT_MAGIC), ALU.mult, ALU.add))
            y0 = i[:, 1, :].bitcast(F32)
            for k in range(4):
                src = y0 if k == 0 else y
                step(dve.scalar_tensor_tensor(out=u, in0=src, scalar=-0.5, in1=src, op0=ALU.mult, op1=ALU.mult))
                step(dve.tensor_tensor(u, u, v, ALU.mult))
                step(dve.scalar_tensor_tensor(out=rstd[:] if k == 3 else y, in0=u, scalar=1.5, in1=src,
                                              op0=ALU.add, op1=ALU.mult))

        def attention(kind):
            A = kind == "a"
            H, G, DV = (HA, GA, DA) if A else (HB, HB, DB)
            NS = 1 if A else 2
            YC = H * DV // P
            QR, KR = (2, 1) if A else (2, 2)
            KP = G * DV
            YB = 1
            KSTACK = (4 if A else 2) * G
            QSTACK = 4
            PREP = 1 + QR + KR
            FIN = YC + 1
            LEAD, EVERY = PREP + 2, PREP + 2 + FIN
            on = ExitStack()
            with on:
                def T(n, s, dt=F32):
                    return sb(f"{n}_{kind}", s, dt, on=on)

                def N(n):
                    return sem(f"{n}_{kind}")

                xn = T("xn", [P, TPB, D])
                xT = T("xT", [P, SEQ])
                q_hi, q_lo = T("q_hi", [P, 2, SEQ], F32R), T("q_lo", [P, 2, SEQ], F32R)
                k_hi, k_lo = T("k_hi", [P, SEQ], F32R), T("k_lo", [P, SEQ], F32R)
                q_stack = T("q_stack", [P, H * NS, SEQ], F32R)
                k_max, k_exp = T("k_max", [P, G, SEQ], F32R), T("k_exp", [P, G, SEQ], F32R)
                v = T("v", [P, TPB, G, DV + 1])
                prob = T("prob", [P, 2, 1280])
                mx = T("mx", [P, TPB, H])
                neg_max = T("neg_max", [H, SEQ], F32R)
                select = T("select", [H, H * P], F32R)
                rsum = T("rsum", [P, 2, TPB])
                y = T("y", [P, TPB, H, DV])
                yT = T("yT", [P, YC, SEQ])
                wq = T("wq", [P, QR * P])
                wk = T("wk", [P, KR * KP])
                wv = T("wv", [P, G * DV])
                wo = T("wo", [P, YC * D])
                ln = norm_scratch(on, kind)
                sel_raw = T("sel_raw", [H, H * P])
                if A:
                    wq_t, wku = T("wq_t", [P, HA, D]), T("wku", [P, DA])
                    wvu, wo_r = T("wvu", [P, DA]), T("wo_r", [P, HA, D])
                else:
                    cos, sin = T("cos", [P, SEQ]), T("sin", [P, SEQ])
                    rot = T("rot", [P, 3, SEQ])
                ps_s = [psum(f"s{i}{kind}", on) for i in range(3)]
                ps_st = [psum(f"st{i}{kind}", on) for i in range(3)]
                ps_y = psum(f"y{kind}", on)
                ps_m = psum(f"m{kind}", on)

                w_in, w_ps, w_done, stat_step = N("w_in"), N("w_ps"), N("w_done"), N("stat_step")
                loads = [(sel_raw[:], io["select"][0:H, 0:H, :].rearrange("k h p -> k (h p)"))]
                if A:
                    loads += [(wq_t[:], io["a_wq_t"].rearrange("(h k) d -> k h d", k=P)), (wku[:], io["a_wku_t"]),
                              (wvu[:], io["a_wvu_t"]), (wo_r[:], io["a_wo"].rearrange("(h k) d -> k h d", k=P)),
                              (wk[:], io["a_wk"]), (wv[:], io["a_wv"])]
                else:
                    loads += [(wq[:], io["b_wq"]), (wk[:], io["b_wk"]), (wv[:], io["b_wv"]), (wo[:], io["b_wo"]),
                              (cos[:], io["rope_cos"]), (sin[:], io["rope_sin"])]
                with nc.Block() as block:
                    @block.sync
                    def _(sp):
                        for dst, src in loads:
                            sp.dma_start(dst, src).then_inc(w_in, 16)

                    @block.vector
                    def _(dve):
                        norm_stats(dve, ln, chain(dve, stat_step))
                        dve.memset(v[:], 1.0).then_inc(w_done, 1)
                        dve.wait_ge(w_in, 16 * len(loads))
                        dve.tensor_copy(select[:], sel_raw[:]).then_inc(w_done, 1)
                        if A:
                            dve.wait_ge(w_ps, 1)
                            dve.tensor_scalar(wq[:], ps_s[0][:, 0:QR * P], HDA ** -0.5, None, ALU.mult).then_inc(w_done, 1)
                            dve.tensor_copy(wo[:], ps_s[1][:, 0:YC * D]).then_inc(w_done, 1)

                    if A:
                        @block.tensor
                        def _(pe):
                            pe.wait_ge(w_in, 16 * len(loads))
                            for h in range(HA):
                                pe.matmul(ps_s[0][:, bass.ts(h, DA)], wq_t[:, h, :], wku[:], start=True, stop=True)
                            for h in range(HA):
                                j, c = h % 4, h // 4
                                mm = pe.matmul(ps_s[1][DA * j:DA * j + DA, bass.ts(c, D)], wvu[:], wo_r[:, h, :],
                                               start=True, stop=True)
                            mm.then_inc(w_ps, 1)

                xn_ready = N("xn_ready")
                m_full, m_free = N("m_full"), N("m_free")
                hi_ready, qk_ready, rot_ready = N("hi_ready"), N("qk_ready"), N("rot_ready")
                v_ready, max_ready = N("v_ready"), N("max_ready")
                q_stacked = [N(f"q_stacked{h}") for h in range(H)]
                k_max_in, k_exp_in = N("k_max_in"), N("k_exp_in")
                s_full, s_free = N("s_full"), N("s_free")
                st_full, st_free = N("st_full"), N("st_free")
                mask_turn = N("mask_turn")
                masked, y_full, y_free, recip = N("masked"), N("y_full"), N("y_free"), N("recip")

                def order(first, last):
                    ahead = [] if last else [("norm", 0)] + [("prep", r) for r in range(PREP)]
                    tail = [("v", 0), ("max_t", 0), ("k_exp", 0)]
                    if first:
                        return (ahead + [("stack", h) for h in range(H)] + [("max", h) for h in range(H)] + tail)
                    steps, maxima = [], list(range(H))
                    per = -(-len(ahead) // max(1, H // 2))
                    for h in range(H):
                        steps += [("exp", h)] + ahead[:per]
                        ahead = ahead[per:]
                        if h >= 1:
                            steps += [("pv", h - 1), ("scale", h - 1)]
                        if not last and h >= H // 2:
                            steps += [("stack", k) for k in range(0 if h == H // 2 else h, h + 1)]
                            while maxima and maxima[0] <= min(h - 1, 2 * (h - H // 2) + 1):
                                steps.append(("max", maxima.pop(0)))
                    steps += [("pv", H - 1), ("scale", H - 1)]
                    if not last:
                        steps += [("max", h) for h in maxima] + tail
                    return steps + [("fin", r) for r in range(FIN)]

                def round_numbers(first, last):
                    uses = [s for s in order(first, last) if s[0] in ("prep", "v", "max_t", "fin")]
                    return {s: n for n, s in enumerate(uses)}

                def rounds_read(s, first, last):
                    at = round_numbers(first, last)
                    return sum(1 for u in at if at[u] < at[s] and u[0] not in ("v", "max_t"))

                def whole(eng, body):
                    body(eng, -1, 0, 0, True, False)
                    with eng.Fori(0, BATCH - 1) as b:
                        body(eng, b, LEAD + EVERY * b, PREP + (PREP + FIN) * b, False, False)
                    body(eng, BATCH - 1, LEAD + EVERY * (BATCH - 1), PREP + (PREP + FIN) * (BATCH - 1), False, True)

                def pe_body(pe, b, base, fbase, first, last):
                    at = round_numbers(first, last)
                    n = b + 1

                    def open_round(s):
                        before = [u for u in at if at[u] == at[s] - 1]
                        if before and before[0][0] == "v":
                            pe.wait_ge(v_ready, n + 1)
                        elif before and before[0][0] == "max_t":
                            pe.wait_ge(max_ready, n + 1)
                        elif first and not before:
                            pass
                        elif before or not first:
                            pe.wait_ge(m_free, fbase + rounds_read(s, first, last))

                    for s in order(first, last):
                        what, h = s
                        g = h * G // H
                        if what == "prep":
                            open_round(s)
                            if h == 0:
                                pe.wait_ge(xn_ready, n + 1)
                                for t in range(TPB):
                                    mm = pe.transpose(ps_m[:, bass.ts(t, P)], xn[:, t, :], ident[:])
                            elif h <= QR:
                                mm = pe.matmul(ps_m[:], wq[:, bass.ts(h - 1, P)], xT[:], start=True, stop=True)
                            else:
                                r = h - 1 - QR
                                mm = pe.matmul(ps_m[0:KP, :], wk[:, r * KP:(r + 1) * KP], xT[:], start=True, stop=True)
                            mm.then_inc(m_full, 1)
                        elif what == "v":
                            open_round(s)
                            for t in range(TPB):
                                mm = pe.matmul(ps_m[:, t * G * DV:(t + 1) * G * DV], xT[:, bass.ts(t, P)], wv[:],
                                               start=True, stop=True)
                            mm.then_inc(m_full, 1)
                        elif what == "max":
                            slot = n * H + h
                            pe.wait_ge(q_stacked[h], 16 * QSTACK * (n + 1))
                            if h == 0:
                                pe.wait_ge(k_max_in, 16 * KSTACK * (n + 1))
                            for qt, need in ((3, 1), (2, 3), (0, None), (1, 4)):
                                bank, col = S_PLACE[qt]
                                if not (first and h == 0) and need:
                                    pe.wait_ge(s_free, 4 * (slot - 1) + need)
                                for a in range(NS):
                                    pe.matmul(ps_s[bank][:, col:col + (qt + 1) * P], q_stack[:, h * NS + a, bass.ts(qt, P)],
                                              k_max[:, g, 0:(qt + 1) * P], start=(a == 0), stop=(a == NS - 1))
                                mm = pe.matmul(ps_s[bank][:, col + qt * P:col + (qt + 1) * P], ident_b[:], causal_b[:],
                                               start=False, stop=True, skip_group_check=True)
                                if qt != 2:
                                    mm.then_inc(s_full, 1)
                        elif what == "max_t":
                            open_round(s)
                            pe.wait_ge(s_free, 4 * H * (n + 1))
                            for qt in range(TPB):
                                mm = pe.transpose(ps_m[0:H, bass.ts(qt, P)], mx[:, qt, :], ident[:])
                            mm.then_inc(m_full, 1)
                        elif what == "exp":
                            slot = b * H + h
                            if h == 0:
                                pe.wait_ge(k_exp_in, 16 * KSTACK * (b + 1))
                                pe.wait_ge(max_ready, b + 1)
                            for kt, bank_no in ((0, 1), (1, 2), (3, 2), (2, 3)):
                                bank, col = ST_PLACE[kt]
                                if kt != 3:
                                    pe.wait_ge(st_free, 3 * slot + bank_no)
                                dst = ps_st[bank][:, col:col + (TPB - kt) * P]
                                for a in range(NS):
                                    pe.matmul(dst, k_exp[:, g, bass.ts(kt, P)], q_stack[:, h * NS + a, kt * P:SEQ],
                                              start=(a == 0), stop=False)
                                mm = pe.matmul(dst, select[:, bass.ts(h, P)], neg_max[:, kt * P:SEQ],
                                               start=False, stop=True)
                                if kt != 1:
                                    mm.then_inc(st_full, 1)
                        elif what == "pv":
                            slot = b * H + h
                            pe.wait_ge(masked, slot + 1)
                            if h == 0:
                                pe.wait_ge(v_ready, b + 1)
                            pe.wait_ge(y_free, slot + 1)
                            for qt in range(TPB):
                                c0 = ((h % YB) * TPB + qt) * (DV + 1)
                                for kt in range(qt + 1):
                                    p0 = P_START[kt] + (qt - kt) * P
                                    mm = pe.matmul(ps_y[:, c0:c0 + DV + 1], prob[:, h % 2, p0:p0 + P], v[:, kt, g, :],
                                                   start=(kt == 0), stop=(kt == qt))
                            mm.then_inc(y_full, 1)
                        elif what == "fin":
                            open_round(s)
                            if h == 0:
                                pe.wait_ge(y_free, H * (b + 1) + YB)
                            if h < YC:
                                for qt in range(TPB):
                                    rows = y[:, qt, :, :].rearrange("p h d -> p (h d)")
                                    mm = pe.transpose(ps_m[:, bass.ts(qt, P)], rows[:, bass.ts(h, P)], ident[:])
                            else:
                                for qt in range(TPB):
                                    for c in range(YC):
                                        mm = pe.matmul(ps_m[:, bass.ts(qt, D)], yT[:, c, bass.ts(qt, P)],
                                                       wo[:, bass.ts(c, D)], start=(c == 0), stop=(c == YC - 1))
                            mm.then_inc(m_full, 1)

                def act_body(act, b, base, fbase, first, last):
                    at = round_numbers(first, last)
                    n = b + 1
                    for s in order(first, last):
                        what, h = s
                        if what == "prep" and h == 0:
                            act.wait_ge(m_full, base + at[s] + 1)
                            act.copy(xT[:], ps_m[:]).then_inc(m_free, 1)
                        elif what == "prep" and (A or h in (QR, QR + KR)):
                            q = h <= QR
                            r = (h - 1) if A else 0
                            dst = q_hi[:, r, :] if q else k_hi[0:KP, :]
                            if not first and q:
                                for k in range(H):
                                    act.wait_ge(q_stacked[k], 16 * QSTACK * n)
                            if not first and not q:
                                act.wait_ge(k_max_in, 16 * KSTACK * n)
                                act.wait_ge(k_exp_in, 16 * KSTACK * n)
                            if A:
                                act.wait_ge(m_full, base + at[s] + 1)
                                act.copy(dst, ps_m[:] if q else ps_m[0:KP, :]).then_inc(hi_ready, 1)
                            else:
                                act.wait_ge(rot_ready, 2 * n + (1 if q else 2))
                                act.copy(dst, rot[:, 2, :]).then_inc(hi_ready, 1)
                        elif what == "v":
                            if not first:
                                act.wait_ge(y_full, 2 + H * n)
                            act.wait_ge(m_full, base + at[s] + 1)
                            act.copy(v[:, :, :, 0:DV], ps_m[:, 0:TPB * G * DV].rearrange(
                                "p (t g d) -> p t g d", t=TPB, g=G)).then_inc(v_ready, 1)
                        elif what == "exp":
                            slot = b * H + h
                            for i, cols in enumerate(BANK_COLS):
                                if i == 0:
                                    act.wait_ge(y_full, slot + 1)
                                act.wait_ge(st_full, 3 * slot + i + 1)
                                act.activation(prob[:, h % 2, i * 512:i * 512 + cols], ps_st[i][:, 0:cols],
                                               ACT.Exp).then_inc(st_free, 1)
                        elif what == "fin" and h < YC:
                            act.wait_ge(m_full, base + at[s] + 1)
                            act.copy(yT[:, h, :], ps_m[:]).then_inc(m_free, 1)

                def dve_body(dve, b, base, fbase, first, last):
                    at = round_numbers(first, last)
                    n = b + 1
                    for s in order(first, last):
                        what, h = s
                        if what == "norm":
                            if not first:
                                dve.wait_ge(m_full, base)
                            for t in range(TPB):
                                tile = bass.ds(n * TPB + t, 1)
                                ins = dve.tensor_scalar(xn[:, t, :], flat(x[:, tile, :]), mean[:, tile], rstd[:, tile],
                                                        ALU.subtract, ALU.mult)
                            ins.then_inc(xn_ready, 1)
                        elif what == "prep" and h > 0:
                            q = h <= QR
                            rows = P if q else KP
                            src = ps_m[0:rows, :]
                            dve.wait_ge(m_full, base + at[s] + 1)
                            if A:
                                hi, lo = (q_hi[:, h - 1, :], q_lo[:, h - 1, :]) if q else (k_hi[0:KP, :], k_lo[0:KP, :])
                                dve.wait_ge(hi_ready, 3 * n + h)
                                dve.tensor_tensor(lo, src, hi.bitcast(F32), ALU.subtract).then_inc(m_free, 1)
                            elif h in (1, 3):
                                if not (first and h == 1):
                                    dve.wait_ge(hi_ready, 2 * n + h // 2)
                                dve.tensor_tensor(rot[:, 0, :], src, cos[:], ALU.mult).then_inc(m_free, 1)
                            else:
                                dve.tensor_tensor(rot[:, 1, :], src, sin[:], ALU.mult).then_inc(m_free, 1)
                                dve.wait_ge(m_free, fbase + rounds_read(s, first, last) + 1)
                                dve.tensor_tensor(rot[:, 2, :], rot[:, 0, :], rot[:, 1, :], ALU.add).then_inc(rot_ready, 1)
                                hi, lo = (q_hi[:, 0, :], q_lo[:, 0, :]) if q else (k_hi[:], k_lo[:])
                                dve.wait_ge(rot_ready, 2 * n + h // 2)
                                dve.wait_ge(hi_ready, 2 * n + h // 2)
                                dve.tensor_tensor(lo, rot[:, 2, :], hi.bitcast(F32), ALU.subtract).then_inc(qk_ready, 1)
                        elif what == "max":
                            slot = n * H + h
                            for qt, full in ((3, 1), (2, 2), (0, 2), (1, 3)):
                                bank, col = S_PLACE[qt]
                                dve.wait_ge(s_full, 3 * slot + full)
                                dve.tensor_reduce(mx[:, qt, h:h + 1], ps_s[bank][:, col:col + (qt + 1) * P], AX_X,
                                                  ALU.max).then_inc(s_free, 1)
                        elif what == "max_t":
                            dve.wait_ge(m_full, base + at[s] + 1)
                            dve.tensor_scalar(neg_max[:], ps_m[0:H, :], -1.0, None, ALU.mult)\
                               .then_inc(max_ready, 1)
                        elif what == "scale":
                            slot = b * H + h
                            c0 = (h % YB) * TPB * (DV + 1)
                            out = ps_y[:, c0:c0 + TPB * (DV + 1)].rearrange("p (t d) -> p t d", t=TPB)
                            dve.wait_ge(y_full, slot + 3)
                            dve.reciprocal(rsum[:, h % 2, :], out[:, :, DV]).then_inc(recip, 1)
                            dve.wait_ge(recip, slot + 1)
                            if h == 0:
                                dve.wait_ge(m_full, base)
                            dve.tensor_tensor(y[:, :, h, :], out[:, :, 0:DV],
                                              rsum[:, h % 2, :].unsqueeze(2).to_broadcast([P, TPB, DV]),
                                              ALU.mult).then_inc(y_free, 1)
                        elif what == "fin" and h == YC:
                            dve.wait_ge(m_full, base + at[s] + 1)
                            tiles = x[:, bass.ds(b * TPB, TPB), :].rearrange("p t d -> p (t d)")
                            dve.tensor_tensor(tiles, tiles, ps_m[:], ALU.add).then_inc(m_free, 1)

                def pool_body(pool, b, base, fbase, first, last):
                    for what, h in order(first, last):
                        if what == "exp":
                            slot = b * H + h
                            pool.wait_ge(st_free, 3 * slot + 6)
                            pool.sem_inc(mask_turn, 1)
                            for c0, step in ((0, 512), (896, P)):
                                ends = prob[:, h % 2, c0:c0 + 2 * step].rearrange("p (a n) -> p a n", a=2)[:, :, 0:P]
                                ins = pool.affine_select(out=ends, in_=ends, compare_op=ALU.is_ge, fill=0.0, base=0,
                                                         pattern=[[0, 2], [1, P]], channel_multiplier=-1)
                            ins.then_inc(masked, 1)

                def stack_keys(sp, dst, s):
                    for g in range(G):
                        src = slice(g * DV, (g + 1) * DV)
                        parts = (k_hi, k_hi, k_lo, k_lo) if A else (k_hi, k_lo)
                        for j, part in enumerate(parts):
                            sp.dma_start(dst[j * DV:(j + 1) * DV, g, :].bitcast(F32), part[src, :].bitcast(F32)).then_inc(s, 16)

                def sp_body(sp, b, base, fbase, first, last):
                    n = b + 1
                    for what, h in order(first, last):
                        if what == "stack":
                            if h == 0:
                                if A:
                                    sp.wait_ge(m_free, fbase + PREP)
                                else:
                                    sp.wait_ge(qk_ready, 2 * (n + 1))
                                if not first:
                                    sp.wait_ge(s_full, 3 * H * n)
                                stack_keys(sp, k_max, k_max_in)
                            if not first:
                                sp.wait_ge(st_full, 3 * (b * H + h + 1))
                            src = slice((h % 4) * DV, (h % 4 + 1) * DV)
                            if A:
                                for j, part in enumerate((q_hi, q_lo, q_hi, q_lo)):
                                    sp.dma_start(q_stack[j * DV:(j + 1) * DV, h, :].bitcast(F32), part[src, h // 4, :].bitcast(F32))\
                                      .then_inc(q_stacked[h], 16)
                            else:
                                for a, part in enumerate((q_hi, q_lo)):
                                    for j in range(2):
                                        sp.dma_start(q_stack[j * DV:(j + 1) * DV, 2 * h + a, :].bitcast(F32), part[src, 0, :].bitcast(F32))\
                                          .then_inc(q_stacked[h], 16)
                        elif what == "k_exp":
                            if not first:
                                sp.wait_ge(st_full, 3 * H * n)
                            stack_keys(sp, k_exp, k_exp_in)

                with nc.Block() as block:
                    @block.tensor
                    def _(pe):
                        pe.sem_inc(y_full, 2)
                        whole(pe, pe_body)

                    @block.scalar
                    def _(act):
                        act.sem_inc(st_free, 3)
                        whole(act, act_body)

                    @block.vector
                    def _(dve):
                        dve.sem_inc(y_free, YB)
                        whole(dve, dve_body)

                    @block.gpsimd
                    def _(pool):
                        whole(pool, pool_body)

                    @block.sync
                    def _(sp):
                        whole(sp, sp_body)


        def each(eng, sequence):
            sequence(0)
            with eng.Fori(1, BATCH) as b:
                sequence(b)

        def after(eng, s, value):
            if not isinstance(value, int):
                eng.wait_ge(s, value)

        def experts(tag, last):
            on = ExitStack()

            def T(n, s, dt=F32, where=on):
                return sb(f"{n}_{tag}", s, dt, on=where)

            def N(n):
                return sem(f"{n}_{tag}")

            with on:
                step_row, step_w = T("step_row", [1, STEPS], I32), T("step_w", [1, STEPS], I32)
                route(tag, T, N, step_row, step_w)
                expert_steps(tag, T, N, step_row, step_w)
            combine(tag, last)

        def route(tag, T_, N, step_row, step_w):
            on = ExitStack()
            with on:
                def T(n, s, dt=F32):
                    return T_(n, s, dt, on)

                rows = T("rows", [P, 2, NT, XROW])
                ln = norm_scratch(on, tag)
                xn, xT = T("xn", [P, TPB, D]), T("xT", [P, SEQ])
                router = T("router", [P, E])
                before, before_b = T("before", [P, P]), T("before_b", [P, P], BF16)
                ones_b = T("ones_b", [P, P], BF16)
                rank_rev, region, carry = T("rank_rev", [P, E, NT]), T("region", [P, E, NT]), T("carry", [P, E, NT])
                step_no, expert_row = T("step_no", [1, STEPS, E]), T("expert_row", [1, E])
                pad = T("pad", [P, XROW])
                dest = T("dest", [P, 2, NT], I32)
                sc, a0, a1 = T("sc", [P, E, NT]), T("a0", [P, E, NT]), T("a1", [P, E, NT])
                hot = [T(f"hot{k}", [P, E, NT]) for k in range(2)]
                both = T("both", [P, E * NT], BF16)
                incl, pos = T("incl", [P, E, NT]), T("pos", [P, E, NT])
                top = [T(f"top{k}", [P, NT]) for k in range(2)]
                r0, r1 = T("r0", [P, NT]), T("r1", [P, NT])
                at_row = T("at_row", [P, 2, NT], U32)
                n_i, n_t, n_c, n_b = T("n_i", [1, 2, E], I32), T("n_t", [1, E]), T("n_c", [1, 2, E]), T("n_b", [1, E])
                one = T("one", [1, E])
                pad_row = T("pad_row", [1, E], I32)
                g0, g1 = T("g0", [1, STEPS, E]), T("g1", [1, STEPS, E])
                s_e, s_c, s_v = T("s_e", [1, STEPS]), T("s_c", [1, STEPS]), T("s_v", [1, STEPS])
                ps_x, ps_l = psum(f"rx{tag}", on), psum(f"rl{tag}", on)
                ps_w, ps_n = psum(f"rw{tag}", on), psum(f"rn{tag}", on)

                c_in, dest_in, dest_set = N("c_in"), N("dest_in"), N("dest_set")
                step = N("route_step")
                normed, copied, x_full, x_read, logits = N("normed"), N("copied"), N("x_full"), N("x_read"), N("logits")
                shifted, scored, counts, counted = N("shifted"), N("scored"), N("counts"), N("counted")
                placed, pads_known, pads_in, rows_in = N("placed"), N("pads_known"), N("pads_in"), N("rows_in")

                def over_e(t):
                    return t.unsqueeze(1).to_broadcast([P, E, NT])

                def by_t(t):
                    return t.rearrange("p e t -> p t e")

                with nc.Block() as block:
                    @block.sync
                    def _(sp):
                        for dst, src in ((router[:], io["router"]), (before[:], io["before"]),
                                         (rank_rev[:], io["rank_rev"].rearrange("p (e t) -> p e t", e=E)),
                                         (region[:], io["region"].rearrange("p (e t) -> p e t", e=E)),
                                         (carry[:], io["carry"].rearrange("p (e t) -> p e t", e=E)),
                                         (step_no[:], io["step_no"].rearrange("p (s e) -> p s e", e=E)),
                                         (expert_row[:], io["expert_row"]), (pad[:], io["pad"])):
                            sp.dma_start(dst, src).then_inc(c_in, 16)
                        sp.dma_start(dest[:], io["dest"]).then_inc(dest_in, 16)
                        sp.wait_ge(c_in, 16 * 8)
                        sp.dma_start(gathered[DUMMY_ROW:ROWS, :], pad[:]).then_inc(pads_in, 16)
                        sp.wait_ge(pads_known, 1)
                        for e in range(E):
                            r = sp.value_load(pad_row[0:1, e:e + 1], min_val=e * REGION, max_val=e * REGION + TOKENS)
                            sp.dma_start(gathered[bass.ds(r, P), :], pad[:]).then_inc(pads_in, 16)
                        sp.wait_ge(pads_in, 16 * (E + 1))

                    @block.tensor
                    def _(pe):
                        pe.wait_ge(c_in, 16 * 8)
                        def sequence(b):
                            pe.wait_ge(normed, b + 1)
                            after(pe, x_read, b)
                            for t in range(TPB):
                                mm = pe.transpose(ps_x[:, bass.ts(t, P)], xn[:, t, :], ident[:])
                            mm.then_inc(x_full, 1)
                            pe.wait_ge(x_read, b + 1)
                            for t in range(TPB):
                                mm = pe.matmul(ps_l[:, bass.ds((b * TPB + t) * E, E)], xT[:, bass.ts(t, P)], router[:],
                                               start=True, stop=True)
                            mm.then_inc(logits, 1)
                        each(pe, sequence)
                        pe.wait_ge(counts, 1)
                        pe.matmul(ps_w[:, 0:E * NT], before_b[:], both[:], start=True, stop=True)
                        pe.matmul(ps_n[:, 0:E * NT], ones_b[:], both[:], start=True, stop=True).then_inc(counted, 1)

                    @block.scalar
                    def _(act):
                        def sequence(b):
                            act.wait_ge(x_full, b + 1)
                            after(act, logits, b)
                            act.copy(xT[:], ps_x[:]).then_inc(x_read, 1)
                        each(act, sequence)
                        act.wait_ge(shifted, 1)
                        act.activation(sc[:], a0[:], ACT.Exp).then_inc(scored, 1)

                    @block.vector
                    def _(dve):
                        do = chain(dve, step)
                        norm_stats(dve, ln, do)

                        def sequence(b):
                            after(dve, x_full, b)
                            after(dve, copied, b)
                            for t in range(TPB):
                                tile = bass.ds(b * TPB + t, 1)
                                ins = dve.tensor_scalar(xn[:, t, :], flat(x[:, tile, :]), mean[:, tile],
                                                        rstd[:, tile], ALU.subtract, ALU.mult)
                            ins.then_inc(normed, 1)
                        each(dve, sequence)
                        dve.wait_ge(c_in, 16 * 8)
                        dve.wait_ge(dest_in, 16)
                        dve.tensor_copy(rows[:, :, :, D].bitcast(I32), dest[:]).then_inc(dest_set, 1)
                        dve.memset(ones_b[:], 1.0)
                        dve.memset(one[:], 1.0)
                        do(dve.tensor_copy(before_b[:], before[:]))
                        dve.wait_ge(logits, BATCH)
                        lg = ps_l[:, 0:E * NT].rearrange("p (t e) -> p t e", e=E)
                        do(dve.tensor_reduce(r0[:], lg, AX_X, ALU.max))
                        dve.tensor_tensor(a0[:], lg.rearrange("p t e -> p e t"), over_e(r0[:]), ALU.subtract).then_inc(shifted, 1)
                        dve.wait_ge(scored, 1)
                        do(dve.tensor_reduce(r0[:], by_t(sc[:]), AX_X, ALU.add))
                        do(dve.reciprocal(r1[:], r0[:]))
                        do(dve.tensor_tensor(sc[:], sc[:], over_e(r1[:]), ALU.mult))
                        for k in range(2):
                            do(dve.tensor_reduce(top[k][:], by_t(sc[:]), AX_X, ALU.max))
                            do(dve.tensor_tensor(a0[:], sc[:], over_e(top[k][:]), ALU.is_equal))
                            do(dve.tensor_tensor(a0[:], a0[:], rank_rev[:], ALU.mult))
                            do(dve.tensor_reduce(r0[:], by_t(a0[:]), AX_X, ALU.max))
                            do(dve.tensor_tensor(hot[k][:], a0[:], over_e(r0[:]), ALU.is_equal))
                            if k == 0:
                                do(dve.scalar_tensor_tensor(out=sc[:], in0=hot[0][:], scalar=-2.0, in1=sc[:],
                                                            op0=ALU.mult, op1=ALU.add))
                        dve.tensor_tensor(both[:].rearrange("p (e t) -> p e t", e=E), hot[0][:], hot[1][:], ALU.add).then_inc(counts, 1)
                        do(dve.tensor_tensor(r0[:], top[0][:], top[1][:], ALU.add))
                        do(dve.tensor_scalar(r0[:], r0[:], TOPK_EPS, None, ALU.add))
                        do(dve.reciprocal(r1[:], r0[:]))
                        for k in range(2):
                            do(dve.tensor_tensor(weight[:, k, :], top[k][:], r1[:], ALU.mult))
                        dve.wait_ge(counted, 1)
                        tot = ps_n[:, 0:E * NT]
                        do(dve.tensor_tensor_scan(incl[:].rearrange("p e t -> p (e t)"), carry[:].rearrange("p e t -> p (e t)"),
                                                  tot, 0.0, ALU.mult, ALU.add))
                        do(dve.tensor_tensor(pos[:], incl[:], tot.rearrange("p (e t) -> p e t", e=E), ALU.subtract))
                        do(dve.tensor_tensor(pos[:], pos[:], ps_w[:, 0:E * NT].rearrange("p (e t) -> p e t", e=E), ALU.add))
                        do(dve.tensor_tensor(pos[:], pos[:], region[:], ALU.add))
                        for k in range(2):
                            do(dve.tensor_tensor(a0[:], hot[k][:], pos[:], ALU.mult))
                            do(dve.tensor_reduce(r0[:], by_t(a0[:]), AX_X, ALU.add))
                            ins = dve.tensor_copy(at_row[:, k, :], r0[:])
                            if k == 0:
                                do(ins)
                        ins.then_inc(placed, 1)
                        n_e = incl[0:1, :, NT - 1]
                        do(dve.tensor_tensor(n_b[:], n_e, expert_row[:], ALU.add))
                        dve.tensor_copy(pad_row[:], n_b[:]).then_inc(pads_known, 1)
                        do(dve.tensor_scalar(n_i[:, 0, :], n_e, float(P - 1), None, ALU.add))
                        do(dve.tensor_scalar(n_i[:, 1, :], n_i[:, 0, :], 7, None, ALU.logical_shift_right))
                        do(dve.tensor_copy(n_t[:], n_i[:, 1, :]))
                        do(dve.tensor_tensor_scan(n_c[:, 0, :], one[:], n_t[:], 0.0, ALU.mult, ALU.add))
                        do(dve.tensor_tensor(n_c[:, 1, :], n_c[:, 0, :], n_t[:], ALU.subtract))
                        first_tile = n_c[:, 1, :].unsqueeze(1).to_broadcast([1, STEPS, E])
                        do(dve.tensor_tensor(g0[:], step_no[:], first_tile, ALU.is_ge))
                        do(dve.tensor_tensor(g1[:], g0[:], first_tile, ALU.mult))
                        do(dve.tensor_reduce(s_e[:], g0[:], AX_X, ALU.add))
                        do(dve.tensor_reduce(s_c[:], g1[:], AX_X, ALU.max))
                        do(dve.tensor_scalar(s_e[:], s_e[:], -1.0, None, ALU.add))
                        do(dve.tensor_tensor(s_c[:], step_no[:, :, 0], s_c[:], ALU.subtract))
                        do(dve.tensor_scalar(s_c[:], s_c[:], float(P), float(-DUMMY_ROW), ALU.mult, ALU.add))
                        do(dve.scalar_tensor_tensor(out=s_c[:], in0=s_e[:], scalar=float(REGION), in1=s_c[:],
                                                    op0=ALU.mult, op1=ALU.add))
                        do(dve.tensor_scalar(s_v[:], step_no[:, :, 0], n_c[:, 0, E - 1:E], None, ALU.is_lt))
                        do(dve.tensor_tensor(s_c[:], s_c[:], s_v[:], ALU.mult))
                        do(dve.tensor_scalar(step_row[:], s_c[:], float(DUMMY_ROW), None, ALU.add))
                        do(dve.tensor_scalar(step_w[:], s_e[:], float(3 * FF), None, ALU.mult))

                    @block.gpsimd
                    def _(pool):
                        def sequence(b):
                            pool.wait_ge(normed, b + 1)
                            tiles = bass.ds(b * TPB, TPB)
                            pool.tensor_copy(rows[:, 0, tiles, 0:D], xn[:])
                            pool.tensor_copy(rows[:, 1, tiles, 0:D], xn[:]).then_inc(copied, 1)
                        each(pool, sequence)
                        pool.wait_ge(dest_set, 1)
                        pool.wait_ge(copied, BATCH)
                        pool.wait_ge(placed, 1)
                        for t in range(NT):
                            for k in range(2):
                                pool.indirect_dma_start(gathered, bass.IndirectOffsetOnAxis(ap=at_row[:, k, t:t + 1], axis=0),
                                                        rows[:, k, t, :], None).then_inc(rows_in, 16)
                        pool.wait_ge(rows_in, 16 * 2 * NT)

        def expert_steps(tag, T, N, step_row, step_w):
            RING = 4
            on = ExitStack()
            with on:
                xg = T("xg", [P, RING, XROW], F32, on)
                to_row = T("to_row", [P, RING], U32, on)
                y = T("y_out", [P, RING, D], F32, on)
                x_hi, x_lo = T("x_hi", [P, 2, P], F32R, on), T("x_lo", [P, 2, P], F32R, on)
                up, h = T("up", [P, 2, FF], F32, on), T("h", [P, 2, FF], F32, on)
                h_hi, h_lo = T("h_hi", [P, 2, FF], F32R, on), T("h_lo", [P, 2, FF], F32R, on)
                ps_x, ps_h, ps_y = psum(f"ex{tag}", on), psum(f"eh{tag}", on), psum(f"ey{tag}", on)
                ps_u = [psum(f"eu{k}{tag}", on) for k in range(2)]
                ps_g = [psum(f"eg{k}{tag}", on) for k in range(2)]
                x_in = [N(f"x_in{k}") for k in range(RING)]
                out_done = [N(f"out_done{k}") for k in range(RING)]
                xt_full, xh_done, xl_done, row_kept = N("xt_full"), N("xh_done"), N("xl_done"), N("row_kept")
                u_full, g_full, u_done, h_done = N("u_full"), N("g_full"), N("u_done"), N("h_done")
                ht_full, hh_done, hl_done = N("ht_full"), N("hh_done"), N("hl_done")
                y_full, y_done = N("y_full"), N("y_done")

                FIRST, LAST = -1, STEPS + 2
                LOOP = (6, STEPS - 2)

                def whole(eng, part):
                    for t in range(FIRST, LOOP[0]):
                        part(eng, t, t % RING)
                    with eng.Fori(0, (LOOP[1] - LOOP[0]) // RING) as i:
                        for u in range(RING):
                            part(eng, i * RING + (LOOP[0] + u), (LOOP[0] + u) % RING)
                    for t in range(LOOP[1], LAST):
                        part(eng, t, t % RING)

                def live(t, lag):
                    return not isinstance(t, int) or 0 <= t - lag < STEPS

                def sure(eng, s, value):
                    if not isinstance(value, int) or value > 0:
                        eng.wait_ge(s, value)

                def pe_part(pe, t, u):
                    if live(t, -1):
                        k = (u + 1) % RING
                        sure(pe, x_in[k], 16 * ((t + 1) // RING + 1) if isinstance(t, int) else 4 * (t + 1 - k) + 16)
                        sure(pe, xl_done, t + 1)
                        pe.transpose(ps_x[:, 0:P], xg[:, k, 0:D], ident[:]).then_inc(xt_full, 1)
                    if live(t, 0):
                        k = u % 2
                        w = pe.value_load(step_w[0:1, bass.ds(t, 1)], min_val=0, max_val=(E - 1) * 3 * FF)
                        w_g, w_u = bass.ds(w, FF), bass.ds(w + FF, FF)
                        sure(pe, xl_done, t + 1)
                        sure(pe, h_done, t - 1)
                        pe.matmul(ps_u[k][:], x_hi[:, k, :], w_hi[:, w_u], start=True, stop=False)
                        pe.matmul(ps_u[k][:], x_hi[:, k, :], w_lo[:, w_u], start=False, stop=False)
                        pe.matmul(ps_u[k][:], x_lo[:, k, :], w_hi[:, w_u], start=False, stop=True).then_inc(u_full, 1)
                        pe.matmul(ps_g[k][:], x_lo[:, k, :], w_hi[:, w_g], start=True, stop=False)
                        pe.matmul(ps_g[k][:], x_hi[:, k, :], w_hi[:, w_g], start=False, stop=False)
                        pe.matmul(ps_g[k][:], x_hi[:, k, :], w_lo[:, w_g], start=False, stop=True).then_inc(g_full, 1)
                    if live(t, 1):
                        k = (u - 1) % 2
                        sure(pe, h_done, t)
                        sure(pe, hl_done, t - 1)
                        for c in range(FC):
                            mm = pe.transpose(ps_h[:, bass.ts(c, P)], h[:, k, bass.ts(c, P)], ident[:])
                        mm.then_inc(ht_full, 1)
                    if live(t, 2):
                        k = u % 2
                        w = pe.value_load(step_w[0:1, bass.ds(t - 2, 1)], min_val=0, max_val=(E - 1) * 3 * FF)
                        sure(pe, hl_done, t - 1)
                        sure(pe, y_done, t - 2)
                        for c in range(FC):
                            w_d = bass.ds(w + (2 * FF + c * P), P)
                            cols = bass.ts(c, P)
                            pe.matmul(ps_y[:, 0:D], h_hi[:, k, cols], w_hi[:, w_d], start=(c == 0), stop=False)
                            pe.matmul(ps_y[:, 0:D], h_hi[:, k, cols], w_lo[:, w_d], start=False, stop=False)
                            mm = pe.matmul(ps_y[:, 0:D], h_lo[:, k, cols], w_hi[:, w_d], start=False, stop=(c == FC - 1))
                        mm.then_inc(y_full, 1)

                def act_part(act, t, u):
                    if live(t, -1):
                        sure(act, xt_full, t + 2)
                        sure(act, g_full, t)
                        act.copy(x_hi[:, (u + 1) % 2, :], ps_x[:, 0:P]).then_inc(xh_done, 1)
                    if live(t, 0):
                        sure(act, u_full, t + 1)
                        act.copy(up[:, u % 2, :], ps_u[u % 2][:]).then_inc(u_done, 1)
                    if live(t, 1):
                        sure(act, ht_full, t)
                        act.copy(h_hi[:, (u - 1) % 2, :], ps_h[:]).then_inc(hh_done, 1)
                    if live(t, 2):
                        k = (u - 2) % RING
                        sure(act, out_done[k], 16 * ((t - 2) // RING) if isinstance(t, int) else 4 * (t - 2 - k))
                        sure(act, y_full, t - 1)
                        act.copy(y[:, k, :], ps_y[:, 0:D]).then_inc(y_done, 1)

                def dve_part(dve, t, u):
                    if live(t, -1):
                        k = (u + 1) % 2
                        sure(dve, xh_done, t + 2)
                        dve.tensor_tensor(x_lo[:, k, :], ps_x[:, 0:P], x_hi[:, k, :].bitcast(F32), ALU.subtract).then_inc(xl_done, 1)
                    if live(t, 0):
                        k = u % 2
                        sure(dve, u_done, t + 1)
                        sure(dve, g_full, t + 1)
                        sure(dve, ht_full, t - 1)
                        dve.scalar_tensor_tensor(out=h[:, k, :], in0=ps_g[k][:], scalar=0.0, in1=up[:, k, :],
                                                 op0=ALU.max, op1=ALU.mult).then_inc(h_done, 1)
                        sure(dve, out_done[u], 16 * (t // RING) if isinstance(t, int) else 4 * (t - u))
                        dve.tensor_copy(to_row[:, u:u + 1], xg[:, u, D:D + 1].bitcast(U32)).then_inc(row_kept, 1)
                    if live(t, 1):
                        k = (u - 1) % 2
                        sure(dve, hh_done, t)
                        dve.tensor_tensor(h_lo[:, k, :], ps_h[:], h_hi[:, k, :].bitcast(F32), ALU.subtract).then_inc(hl_done, 1)

                def pool_part(pool, t, u):
                    if live(t, 2):
                        k = (u - 2) % RING
                        sure(pool, row_kept, t - 1)
                        sure(pool, y_done, t - 1)
                        pool.sem_inc(out_turn, 1)
                        pool.indirect_dma_start(by_token, bass.IndirectOffsetOnAxis(ap=to_row[:, k:k + 1], axis=0),
                                                y[:, k, :], None, bounds_check=2 * TOKENS - 1, oob_is_err=False)\
                            .then_inc(out_done[k], 16)

                def sp_part(sp, t, u):
                    if live(t, -2):
                        k = (u + 2) % RING
                        r = sp.value_load(step_row[0:1, bass.ds(t + 2, 1)], min_val=0, max_val=DUMMY_ROW)
                        sure(sp, row_kept, t - 1)
                        sp.dma_start(xg[:, k, :], gathered[bass.ds(r, P), :]).then_inc(x_in[k], 16)

                out_turn = N("out_turn")
                with nc.Block() as block:
                    @block.tensor
                    def _(pe):
                        whole(pe, pe_part)

                    @block.scalar
                    def _(act):
                        whole(act, act_part)

                    @block.vector
                    def _(dve):
                        whole(dve, dve_part)

                    @block.gpsimd
                    def _(pool):
                        whole(pool, pool_part)
                        for k in range(RING):
                            pool.wait_ge(out_done[k], 16 * (STEPS // RING))

                    @block.sync
                    def _(sp):
                        sp_part(sp, -2, -2 % RING)
                        whole(sp, sp_part)

        def combine(tag, last):
            on = ExitStack()
            with on:
                parts = sb(f"parts_{tag}", [P, 2, 2, TPB, D], on=on)
                part_in = [sem(f"part_in{k}_{tag}") for k in range(2)]
                first, added, stored = sem(f"first_{tag}"), sem(f"added_{tag}"), sem(f"stored_{tag}")
                src = by_token.rearrange("(k t p) d -> p k t d", k=2, p=P)
                with nc.Block() as block:
                    @block.sync
                    def _(sp):
                        def pair(i):
                            for u in range(2):
                                b = i * 2 + u
                                if not isinstance(i, int):
                                    sp.wait_ge(added, b - 1)
                                for k in range(2):
                                    sp.dma_start(parts[:, u, k, :, :], src[:, k, bass.ds(b * TPB, TPB), :]).then_inc(part_in[u], 16)
                        pair(0)
                        with sp.Fori(1, BATCH // 2) as i:
                            pair(i)

                    @block.vector
                    def _(dve):
                        with dve.Fori(0, BATCH // 2) as i:
                            for u in range(2):
                                b = i * 2 + u
                                dve.wait_ge(part_in[u], 32 * i + 32)
                                for k in range(2):
                                    if k == 1:
                                        dve.wait_ge(first, b + 1)
                                    for t in range(TPB):
                                        tile = bass.ds(b * TPB + t, 1)
                                        ins = dve.scalar_tensor_tensor(
                                            out=flat(x[:, tile, :]), in0=parts[:, u, k, t, :], scalar=flat(weight[:, k:k + 1, tile]),
                                            in1=flat(x[:, tile, :]), op0=ALU.mult, op1=ALU.add)
                                    ins.then_inc(first if k == 0 else added, 1)

                    if last:
                        @block.scalar
                        def _(act):
                            out = io["out"].rearrange("b (t p) d -> p (b t) d", p=P)
                            with act.Fori(0, BATCH) as b:
                                act.wait_ge(added, b + 1)
                                tiles = bass.ds(b * TPB, TPB)
                                act.dma_start(out[:, tiles, :], x[:, tiles, :]).then_inc(stored, 16)
                            act.wait_ge(stored, 16 * BATCH)

        def store_out():
            with nc.Block() as block:
                stored = sem("stored")

                @block.sync
                def _(sp):
                    sp.dma_start(io["out"].rearrange("b (t p) d -> p (b t) d", p=P), x[:]).then_inc(stored, 16)
                    sp.wait_ge(stored, 16)

        setup()
        attention("a")
        if stages >= 2:
            experts("1", last=False)
        if stages >= 3:
            attention("b")
        if stages >= 4:
            experts("2", last=True)
        if stages < 4:
            store_out()


def kernel(L0_attn_a_x, L0_attn_a_wq, L0_attn_a_wk_down, L0_attn_a_wv_down, L0_attn_a_wk_up, L0_attn_a_wv_up,
           L0_attn_a_wo, L0_attn_b_wq, L0_attn_b_wk, L0_attn_b_wv, L0_attn_b_wo, L0_ffn_Wr, L0_ffn_Wg, L0_ffn_Wu,
           L0_ffn_Wd, stages=4):
    import concourse.bacc as bacc
    from concourse.bass_utils import run_bass_kernel_spmd

    arrays = dict(make_constants())
    arrays["x"] = L0_attn_a_x
    arrays["a_wq_t"] = np.transpose(L0_attn_a_wq)
    arrays["a_wku_t"] = np.transpose(L0_attn_a_wk_up)
    arrays["a_wvu_t"] = np.transpose(L0_attn_a_wv_up)
    arrays["a_wo"] = L0_attn_a_wo
    arrays["a_wk"] = L0_attn_a_wk_down
    arrays["a_wv"] = L0_attn_a_wv_down
    pair = np.arange(DB // 2)
    rows = np.concatenate([h * DB + np.concatenate([2 * pair, 2 * pair + 1]) for h in range(HB)])
    swap = np.concatenate([h * DB + np.concatenate([2 * pair + 1, 2 * pair]) for h in range(HB)])
    for name, w in (("b_wq", L0_attn_b_wq), ("b_wk", L0_attn_b_wk)):
        wt = np.transpose(w)
        arrays[name] = np.concatenate([wt[:, rows], wt[:, swap]], axis=1)
    arrays["b_wv"] = np.transpose(L0_attn_b_wv)
    arrays["b_wo"] = np.transpose(L0_attn_b_wo)
    arrays["router"] = np.transpose(L0_ffn_Wr)
    down = np.transpose(np.reshape(L0_ffn_Wd, (E, D, FC, P)), (3, 0, 2, 1)).reshape(P, E, FF)
    arrays["w_ffn"] = np.concatenate([np.transpose(L0_ffn_Wg, (2, 0, 1)), np.transpose(L0_ffn_Wu, (2, 0, 1)), down],
                                     axis=2)
    arrays = {f"in_{k}": np.ascontiguousarray(a) for k, a in arrays.items()}

    nc = bacc.Bacc("TRN2", target_bir_lowering=False, num_devices=1)
    io = {k[3:]: nc.dram_tensor(k, a.shape, mybir.dt.from_np(a.dtype), kind="ExternalInput").ap()
          for k, a in arrays.items()}
    io["out"] = nc.dram_tensor("out", (BATCH, SEQ, D), F32, kind="ExternalOutput").ap()
    build(nc, io, stages)
    r = run_bass_kernel_spmd(nc, [arrays], core_ids=[0])
    return r.results[0]["out"]
```

```python
from contextlib import ExitStack

import numpy as np

import concourse.bass as bass
from concourse import mybir

ALU = mybir.AluOpType
ACT = mybir.ActivationFunctionType
AX_X = mybir.AxisListType.X
F32 = mybir.dt.float32
F32R = mybir.dt.float32r
BF16 = mybir.dt.bfloat16
I32 = mybir.dt.int32
U32 = mybir.dt.uint32

P = 128
BATCH = 8
SEQ = 512
D = 128
TPB = SEQ // P
NT = BATCH * TPB
TOKENS = NT * P
LN_EPS = 1e-5
RSQRT_MAGIC = 0x5F3759DF

HA, GA, DA, HDA = 8, 2, 32, 128
HB, DB = 2, 64
ROPE_BASE = 10000.0

E, FF = 8, 512
FC = FF // P
REGION = TOKENS + P
DUMMY_ROW = E * REGION
ROWS = DUMMY_ROW + P
XROW = D + 1
STEPS = 2 * TOKENS // P + E
NOWHERE = 1 << 20
TOPK_EPS = float(np.finfo(np.float32).eps)
MASKED = -1e30

S_PLACE = [(1, 384), (2, 0), (1, 0), (0, 0)]
ST_PLACE = [(0, 0), (1, 0), (2, 0), (1, 384)]
P_START = [0, 512, 1024, 896]
BANK_COLS = [512, 512, 256]


def make_constants():
    c = {}
    c["ident"] = np.eye(P, dtype=np.float32)
    q, k = np.arange(P)[:, None], np.arange(P)[None, :]
    c["causal"] = np.where(k > q, np.float32(MASKED), np.float32(0)).astype(np.float32)
    c["before"] = (q < k).astype(np.float32)
    sel = np.zeros((HB, HB, P), np.float32)
    for h in range(HB):
        sel[h, h] = 1
    c["select"] = sel
    theta = np.exp((np.log(np.float32(ROPE_BASE)) * np.arange(DB // 2, dtype=np.float32)
                    / np.float32(DB)).astype(np.float64)).astype(np.float32)
    args = (theta[:, None] * np.arange(SEQ, dtype=np.float32)[None, :]).astype(np.float64)
    scale = DB ** -0.25
    c["rope_cos"] = np.tile(np.cos(args) * scale, (2 * HB, 1)).astype(np.float32)
    sin = np.sin(args) * scale
    c["rope_sin"] = np.tile(np.concatenate([-sin, sin]), (HB, 1)).astype(np.float32)
    c["rank_rev"] = np.tile(np.repeat(np.arange(E, 0, -1, dtype=np.float32), TPB), (P, 1))
    c["region"] = np.tile(np.arange(E, dtype=np.float32) * REGION, (P, 1))
    carry = np.ones((E, TPB), np.float32)
    carry[:, 0] = 0
    c["carry"] = np.tile(carry.reshape(1, -1), (P, 1))
    c["step_no"] = np.repeat(np.arange(STEPS, dtype=np.float32), E)[None, :]
    t, p = np.arange(NT)[None, None, :], np.arange(P)[:, None, None]
    c["dest"] = (np.arange(2)[None, :, None] * TOKENS + t * P + p).astype(np.uint32).view(np.int32)
    pad = np.zeros((P, XROW), np.float32)
    pad[:, D] = np.full(P, NOWHERE, np.uint32).view(np.float32)
    c["pad"] = pad
    return c


def flat(ap):
    return ap.rearrange("p a n -> p (a n)")


def wait(eng, s, value):
    if not isinstance(value, int) or value > 0:
        eng.wait_ge(s, value)


def chain(eng, s, base):
    n = [0]

    def link(ins):
        n[0] += 1
        ins.then_inc(s, 1)
        eng.wait_ge(s, base + n[0])

    link.count = n
    return link


def build(nc, io):
    ctx = ExitStack()

    def sb(name, shape, dt=F32, on=ctx):
        return on.enter_context(nc.sbuf_tensor("sb_" + name, shape, dt))

    def psum(name, on):
        return on.enter_context(nc.psum_tensor("ps_" + name, [P, 512], F32))

    def sem(name):
        return ctx.enter_context(nc.semaphore(name))

    with ctx:
        x = sb("x", [P, NT, D])
        w_hi, w_lo = sb("w_hi", [P, E * 2 * FF], F32R), sb("w_lo", [P, E * 2 * FF], F32R)
        w_down = sb("w_down", [P, E * 2 * FF], F32R)
        ident = sb("ident", [P, P])
        ident_b, causal_b = sb("ident_b", [P, P], BF16), sb("causal_b", [P, P], BF16)
        before_b, ones_b = sb("before_b", [P, P], BF16), sb("ones_b", [P, P], BF16)
        router = sb("router", [P, E])
        rank_rev, carry = sb("rank_rev", [P, E, TPB]), sb("carry", [P, E, TPB])
        region = sb("region", [P, E])
        placed_to = sb("placed_to", [P, E])
        pad = sb("pad", [P, XROW])
        dest = sb("dest", [P, 2, NT], I32)
        weight = sb("weight", [P, 2, NT])
        step_row, step_w = sb("step_row", [1, STEPS], I32), sb("step_w", [1, STEPS], I32)

        x_rest = sem("x_rest")
        gathered = nc.dram_tensor("gathered", (ROWS, XROW), F32, kind="Internal").ap()
        by_token = nc.dram_tensor("by_token", (2 * TOKENS, D), F32, kind="Internal").ap()

        def load():
            on = ExitStack()
            with on:
                causal, before = sb("causal", [P, P], on=on), sb("before", [P, P], on=on)
                loaded, converted = sem("loaded"), sem("converted")
                x_src = io["x"].rearrange("b (t p) d -> p (b t) d", p=P)
                loads = [(causal[:], io["causal"]), (before[:], io["before"]), (ident[:], io["ident"]),
                         (x[:, 0:TPB, :], x_src[:, 0:TPB, :]),
                         (router[:], io["router"]), (rank_rev[:], io["rank_rev"].rearrange("p (e t) -> p e t", e=E)),
                         (carry[:], io["carry"].rearrange("p (e t) -> p e t", e=E)), (region[:], io["region"]),
                         (pad[:], io["pad"]), (dest[:], io["dest"])]
                with nc.Block() as block:
                    @block.sync
                    def _(sp):
                        for dst, src in loads:
                            sp.dma_start(dst, src).then_inc(loaded, 16)
                        sp.dma_start(x[:, TPB:, :], x_src[:, TPB:, :]).then_inc(x_rest, 16)
                        sp.wait_ge(loaded, 16 * len(loads))

                    @block.vector
                    def _(dve):
                        dve.memset(ones_b[:], 1.0)
                        dve.wait_ge(loaded, 16 * len(loads))
                        dve.tensor_copy(ident_b[:], ident[:])
                        dve.tensor_copy(causal_b[:], causal[:])
                        dve.tensor_copy(before_b[:], before[:]).then_inc(converted, 1)
                        dve.wait_ge(converted, 1)

        LN_LINKS = 15

        def norm_stats(dve, s, tiles, do):
            st, t, i, mean = s["st"], s["t"], s["i"], s["mean"]
            v, d, y, u = (t[:, k, :] for k in range(4))
            for k in range(TPB):
                ins = dve.bn_stats(st[:, k, :], flat(x[:, bass.ds(tiles + k, 1), :]))
            do(ins)
            dve.tensor_tensor(mean[:], st[:, :, 1], st[:, :, 4], ALU.add)
            dve.tensor_tensor(d, st[:, :, 1], st[:, :, 4], ALU.subtract)
            do(dve.tensor_tensor(v, st[:, :, 2], st[:, :, 5], ALU.add))
            dve.tensor_scalar(mean[:], mean[:], 0.5, None, ALU.mult)
            dve.tensor_scalar(v, v, 1.0 / D, LN_EPS, ALU.mult, ALU.add)
            do(dve.scalar_tensor_tensor(out=u, in0=d, scalar=0.25, in1=d, op0=ALU.mult, op1=ALU.mult))
            do(dve.tensor_tensor(v, v, u, ALU.add))
            do(dve.tensor_scalar(i[:, 0, :], v.bitcast(I32), 1, None, ALU.logical_shift_right))
            do(dve.tensor_scalar(i[:, 1, :], i[:, 0, :], -1.0, float(RSQRT_MAGIC), ALU.mult, ALU.add))
            src = i[:, 1, :].bitcast(F32)
            for k in range(3):
                dst = s["rstd"][:] if k == 2 else (y, d)[k]
                do(dve.scalar_tensor_tensor(out=u, in0=src, scalar=-0.5, in1=src, op0=ALU.mult, op1=ALU.mult))
                do(dve.tensor_tensor(u, u, v, ALU.mult))
                ins = dve.scalar_tensor_tensor(out=dst, in0=u, scalar=1.5, in1=src, op0=ALU.add, op1=ALU.mult)
                src = dst
                do(ins)

        def norm_scratch(T, tag):
            return dict(st=T(f"ln_st_{tag}", [P, TPB, 6]), t=T(f"ln_t_{tag}", [P, 4, TPB]), i=T(f"ln_i_{tag}", [P, 2, TPB], I32),
                        mean=T(f"ln_mean_{tag}", [P, TPB]), rstd=T(f"ln_rstd_{tag}", [P, TPB]))

        def attention(kind):
            A = kind == "a"
            H, G, DV = (HA, GA, DA) if A else (HB, HB, DB)
            NS = 1 if A else 2
            KS = 3 * DV if A else P
            KX = KS + 1 if A else P
            YM = 2 * DV
            YC = H * DV // P
            KR = 1 if A else 2
            QR = 2
            KP = G * DV
            KSTACK = (3 if A else 2) * G
            QSTACK = 3 if A else 4
            PREP = 1 + QR + KR
            ROUTE_LINKS = 26

            def N(n):
                return sem(f"{n}_{kind}")

            on = ExitStack()
            with on:
                def T(n, s, dt=F32):
                    return sb(f"{n}_{kind}", s, dt, on=on)

                wq, wk, wv, wo = T("wq", [P, QR * P]), T("wk", [P, KR * KP]), T("wv", [P, G * DV]), T("wo", [P, YC * D])
                select = None if A else T("select", [H, H * P], F32R)
                v = T("v", [P, 2, TPB * G, 2 * DV])
                w_in, w_ps, w_done = N("w_in"), N("w_ps"), N("w_done")
                with ExitStack() as raws:
                    loads = []
                    if A:
                        wq_t, wo_r = sb("wq_t", [P, HA, D], on=raws), sb("wo_r", [P, HA, D], on=raws)
                        wku, wvu = sb("wku", [P, DA], on=raws), sb("wvu", [P, DA], on=raws)
                        ps_wq, ps_wo = psum("wq", raws), psum("wo", raws)
                        loads += [(wq_t[:], io["a_wq_t"].rearrange("(h k) d -> k h d", k=P)), (wku[:], io["a_wku_t"]),
                                  (wvu[:], io["a_wvu_t"]), (wo_r[:], io["a_wo"].rearrange("(h k) d -> k h d", k=P)),
                                  (wk[:], io["a_wk"]), (wv[:], io["a_wv"])]
                    else:
                        sel_raw = sb(f"sel_raw_{kind}", [H, H * P], on=raws)
                        loads += [(sel_raw[:], io["select"].rearrange("k h p -> k (h p)")), (wq[:], io["b_wq"]), (wk[:], io["b_wk"]), (wv[:], io["b_wv"]), (wo[:], io["b_wo"])]
                    with nc.Block() as block:
                        @block.sync
                        def _(sp):
                            for dst, src in loads:
                                sp.dma_start(dst, src).then_inc(w_in, 16)

                        @block.vector
                        def _(dve):
                            dve.memset(v[:], 1.0).then_inc(w_done, 1)
                            dve.wait_ge(w_in, 16 * len(loads))
                            if not A:
                                dve.tensor_copy(select[:], sel_raw[:]).then_inc(w_done, 1)
                            else:
                                dve.wait_ge(w_ps, 1)
                                dve.tensor_scalar(wq[:], ps_wq[:, 0:QR * P], HDA ** -0.5, None, ALU.mult).then_inc(w_done, 1)
                                dve.tensor_copy(wo[:], ps_wo[:, 0:YC * D]).then_inc(w_done, 1)

                        if A:
                            @block.tensor
                            def _(pe):
                                pe.wait_ge(w_in, 16 * len(loads))
                                for h in range(HA):
                                    pe.matmul(ps_wq[:, bass.ts(h, DA)], wq_t[:, h, :], wku[:], start=True, stop=True)
                                for h in range(HA):
                                    j, c = h % 4, h // 4
                                    mm = pe.matmul(ps_wo[DA * j:DA * j + DA, bass.ts(c, D)], wvu[:], wo_r[:, h, :],
                                                   start=True, stop=True)
                                mm.then_inc(w_ps, 1)

                xn, xT = T("xn", [P, TPB, D]), T("xT", [P, SEQ])
                q_hi, q_lo = T("q_hi", [P, 2 if A else 1, SEQ], F32R), T("q_lo", [P, 2 if A else 1, SEQ], F32R)
                k_hi, k_lo = T("k_hi", [P, SEQ], F32R), T("k_lo", [P, SEQ], F32R)
                q_stack = T("q_stack", [P, 2, H * NS, SEQ], F32R)
                k_stack = T("k_stack", [P, 2, G, SEQ], F32R)
                prob = T("prob", [P, 2, 1280])
                mx = T("mx", [P, TPB, H])
                neg_max = T("neg_max", [H, 1 if A else 2, SEQ], F32R)
                y_sum, yT = T("y_sum", [P, YC, SEQ]), T("yT", [P, YC, SEQ])
                ln, rn = norm_scratch(T, "x"), norm_scratch(T, "r")
                if A:
                    w_raw = T("w_raw", [P, FF])
                else:
                    cos, sin, rot = T("cos", [P, SEQ]), T("sin", [P, SEQ]), T("rot", [P, 3, SEQ])
                    parts = T("parts", [P, 2, 2, TPB, D])
                rows = T("rows", [P, 2, TPB, XROW])
                sc, a0, a1 = T("sc", [P, E, TPB]), T("a0", [P, E, TPB]), T("a1", [P, E, TPB])
                hot = [T(f"hot{k}", [P, E, TPB]) for k in range(2)]
                both = T("both", [P, E * TPB], BF16)
                incl, pos = T("incl", [P, E, TPB]), T("pos", [P, E, TPB])
                top = [T(f"top{k}", [P, TPB]) for k in range(2)]
                r0, r1 = T("r0", [P, TPB]), T("r1", [P, TPB])
                at_row = T("at_row", [P, 2, TPB], U32)

                ps_s = [psum(f"s{i}{kind}", on) for i in range(3)]
                ps_st = [psum(f"st{i}{kind}", on) for i in range(3)]
                ps_y, ps_m = psum(f"y{kind}", on), psum(f"m{kind}", on)

                xn_ready, ln_step, ln_turn = N("xn_ready"), N("ln_step"), N("ln_turn")
                m_full, m_free = N("m_full"), N("m_free")
                hi_ready, k_stacked = N("hi_ready"), N("k_stacked")
                v_ready, max_ready = N("v_ready"), N("max_ready")
                q_stacked = [N(f"q_stacked{h}") for h in range(H)]
                s_full, s_free = N("s_full"), N("s_free")
                st_full, st_free, masked = N("st_full"), N("st_free"), N("masked")
                y_ready = N("y_ready")
                y_full, y_free, recip = N("y_full"), N("y_free"), N("recip")
                mask_turn, load_turn = N("mask_turn"), N("load_turn")
                if A:
                    max_in, ones_set = N("max_in"), N("ones_set")
                    raw_in, raw_step, raw_split = N("raw_in"), N("raw_step"), N("raw_split")
                else:
                    rot_ready, lo_ready, rope_in = N("rot_ready"), N("lo_ready"), N("rope_in")
                    part_in, part_step = [N("part_in0"), N("part_in1")], N("part_step")
                r_normed, r_step, r_shifted, r_scored = N("r_normed"), N("r_step"), N("r_shifted"), N("r_scored")
                r_counts, r_placed, r_turn, rows_in, rows_free, r_copied = N("r_counts"), N("r_placed"), N("r_turn"), N("rows_in"), N("rows_free"), N("r_copied")

                FIRST, START, MID, LATE, END, AFTER = range(6)

                if A:
                    ORDER = (("stats", 0), ("norm", 0), ("prep", 0), ("exp", 0), ("scale", 1), ("prep", 1),
                             ("exp", 1), ("prep", 2), ("prep", 3), ("stack", 0), ("fin", 0), ("pv", 0), ("v", 0),
                             ("stats", 1), ("norm", 1), ("exp", 2), ("pv", 1), ("r_stats", 0), ("exp", 3),
                             ("max", 0), ("pv", 2), ("r_norm", 0), ("route", 0), ("route", 1), ("max", 1),
                             ("exp", 4), ("pv", 3), ("choose", 0), ("max", 2), ("exp", 5), ("pv", 4), ("choose", 1),
                             ("max", 3), ("exp", 6), ("pv", 5), ("route", 2), ("max", 4), ("scatter", 0), ("exp", 7),
                             ("scale", 0), ("max", 5), ("scatter", 1), ("pv", 6), ("max", 6), ("scatter", 2),
                             ("max", 7), ("max_t", 0), ("scatter", 3), ("pv", 7), ("free", 0))
                else:
                    ORDER = (("stats", 0), ("norm", 0), ("prep", 0), ("exp", 0), ("scale", 0), ("prep", 1),
                             ("prep", 2), ("exp", 1), ("prep", 3), ("prep", 4), ("stack", 0), ("fin", 0), ("pv", 0),
                             ("v", 0), ("r_stats", 0), ("pv", 1), ("r_norm", 0), ("route", 0), ("route", 1),
                             ("choose", 0), ("max", 0), ("choose", 1), ("max", 1), ("max_t", 0), ("route", 2),
                             ("stats", 1), ("norm", 1), ("scatter", 0), ("scatter", 1), ("scatter", 2),
                             ("scatter", 3), ("free", 0))
                NEXT = ("prep", "stack", "v", "max", "max_t")
                NOW = ("exp", "pv")
                ROUTED = ("fin", "r_stats", "r_norm", "route", "choose", "scatter", "free")

                def order(part):
                    def takes_part(s):
                        what, h = s
                        if what in ("stats", "norm"):
                            return part == FIRST if h == 0 else part <= MID
                        if what == "scale":
                            return part >= MID if h == YC - 1 else START <= part <= END
                        return (part <= LATE if what in NEXT else START <= part <= END if what in NOW else part >= MID)
                    return [s for s in ORDER if takes_part(s)]

                RAW = (("prep", 0), ("stack", 0), ("max", 3))
                OWN = ("v", "max_t")
                IN_ROUND = ("prep", "v", "max_t", "fin", "route")

                def is_round(s):
                    return s[0] in IN_ROUND

                def numbers(part):
                    n = f = 0
                    at = {}
                    for s in order(part):
                        if is_round(s):
                            at[s] = (n, f)
                            n += 1
                            f += s[0] not in OWN
                    return at, n, f

                TOTALS = [numbers(p)[1:] for p in range(6)]

                def bases(part, b):
                    out = []
                    for k in range(2):
                        c = [t[k] for t in TOTALS]
                        out.append({FIRST: 0, START: c[0], MID: c[0] + c[1] + c[2] * (b - 1),
                                    LATE: c[0] + c[1] + c[2] * (BATCH - 3), END: c[0] + c[1] + c[2] * (BATCH - 3) + c[3],
                                    AFTER: c[0] + c[1] + c[2] * (BATCH - 3) + c[3] + c[4]}[part])
                    return out

                def whole(eng, body):
                    body(eng, -1, FIRST, 1, 0)
                    body(eng, 0, START, 0, 1)
                    with eng.Fori(0, (BATCH - 4) // 2) as i:
                        for u in (1, 2):
                            body(eng, i * 2 + u, MID, u % 2, (u + 1) % 2)
                    for b, part in ((BATCH - 3, MID), (BATCH - 2, LATE), (BATCH - 1, END), (BATCH, AFTER)):
                        body(eng, b, part, b % 2, (b + 1) % 2)

                def pe_body(pe, b, part, pb, pn):
                    at, _, _ = numbers(part)
                    full, free = bases(part, b)
                    n, r = b + 1, b - 1
                    steps = order(part)
                    rounds = [s for s in steps if is_round(s)]

                    def open_round(s):
                        k = rounds.index(s)
                        before = rounds[k - 1][0] if k else None
                        if before == "v":
                            pe.wait_ge(v_ready, n + 1)
                        elif before == "max_t":
                            pe.wait_ge(max_ready, n + 1)
                        else:
                            if k == 0 and START <= part <= END:
                                pe.wait_ge(max_ready, b + 1)
                            wait(pe, m_free, free + at[s][1])

                    for s in steps:
                        what, h = s
                        g = h * G // H
                        if is_round(s):
                            open_round(s)
                        if what == "prep":
                            if h == 0:
                                pe.wait_ge(xn_ready, n + 1)
                                for t in range(TPB):
                                    mm = pe.transpose(ps_m[:, bass.ts(t, P)], xn[:, t, :], ident[:])
                            elif h <= QR:
                                mm = pe.matmul(ps_m[:], wq[:, bass.ts(h - 1, P)], xT[:], start=True, stop=True)
                            else:
                                k = h - 1 - QR
                                mm = pe.matmul(ps_m[0:KP, :], wk[:, k * KP:(k + 1) * KP], xT[:], start=True, stop=True)
                            mm.then_inc(m_full, 1)
                        elif what == "v":
                            for t in range(TPB):
                                mm = pe.matmul(ps_m[:, t * G * DV:(t + 1) * G * DV], xT[:, bass.ts(t, P)], wv[:],
                                               start=True, stop=True)
                            mm.then_inc(m_full, 1)
                        elif what == "max":
                            slot = n * H + h
                            pe.wait_ge(q_stacked[h], 16 * QSTACK * (n + 1))
                            if h == 0:
                                pe.wait_ge(k_stacked, 16 * KSTACK * (n + 1))
                            for qt, need in ((3, 1), (2, 3), (0, None), (1, 4)):
                                bank, col = S_PLACE[qt]
                                if need:
                                    wait(pe, s_free, 4 * (slot - 1) + need)
                                for a in range(NS):
                                    pe.matmul(ps_s[bank][:, col:col + (qt + 1) * P], q_stack[0:KS, pn, h * NS + a, bass.ts(qt, P)],
                                              k_stack[0:KS, pn, g, 0:(qt + 1) * P], start=(a == 0), stop=(a == NS - 1))
                                mm = pe.matmul(ps_s[bank][:, col + qt * P:col + (qt + 1) * P], ident_b[:], causal_b[:],
                                               start=False, stop=True, skip_group_check=True)
                                if qt != 2:
                                    mm.then_inc(s_full, 1)
                        elif what == "max_t":
                            pe.wait_ge(s_free, 4 * H * (n + 1))
                            for qt in range(TPB):
                                mm = pe.transpose(ps_m[0:H, bass.ts(qt, P)], mx[:, qt, :], ident[:])
                            mm.then_inc(m_full, 1)
                        elif what == "exp":
                            slot = b * H + h
                            if h == 0:
                                if A:
                                    pe.wait_ge(max_in, 16 * (b + 1))
                                else:
                                    pe.wait_ge(max_ready, b + 1)
                            for kt, bank_no in ((0, 1), (1, 2), (3, None), (2, 3)):
                                bank, col = ST_PLACE[kt]
                                if bank_no:
                                    wait(pe, st_free, 3 * (slot - 1) + bank_no)
                                dst = ps_st[bank][:, col:col + (TPB - kt) * P]
                                for a in range(NS):
                                    mm = pe.matmul(dst, k_stack[0:KX, pb, g, bass.ts(kt, P)],
                                                   q_stack[0:KX, pb, h * NS + a, kt * P:SEQ], start=(a == 0), stop=A)
                                if not A:
                                    mm = pe.matmul(dst, select[:, bass.ts(h, P)], neg_max[:, pb, kt * P:SEQ],
                                                   start=False, stop=True)
                                if kt != 1:
                                    mm.then_inc(st_full, 1)
                        elif what == "pv":
                            slot = b * H + h
                            pe.wait_ge(masked, slot + 1)
                            if h == 0:
                                pe.wait_ge(v_ready, b + 1)
                            wait(pe, y_free, slot - 1 if A else slot)
                            y0 = (h % 2) * YM if A else 0
                            for kt in range(TPB):
                                mm = pe.matmul(ps_y[y0:y0 + YM, kt * P:SEQ], v[:, pb, kt * G + g, :],
                                               prob[:, h % 2, P_START[kt]:P_START[kt] + (TPB - kt) * P],
                                               start=(kt == 0), stop=(kt == TPB - 1), skip_group_check=True)
                            mm.then_inc(y_full, 1)
                        elif what == "fin":
                            pe.wait_ge(y_ready, YC * (r + 1))
                            for qt in range(TPB):
                                for c in range(YC):
                                    mm = pe.matmul(ps_m[:, bass.ts(qt, D)], yT[:, c, bass.ts(qt, P)],
                                                   wo[:, bass.ts(c, D)], start=(c == 0), stop=(c == YC - 1))
                            mm.then_inc(m_full, 1)
                        elif what == "route" and h == 0:
                            pe.wait_ge(r_normed, r + 1)
                            for t in range(TPB):
                                mm = pe.transpose(ps_m[:, bass.ts(t, P)], rows[:, 0, t, 0:D], ident[:])
                            mm.then_inc(m_full, 1)
                        elif what == "route" and h == 1:
                            for t in range(TPB):
                                mm = pe.matmul(ps_m[:, bass.ts(t, E)], xT[:, bass.ts(t, P)], router[:], start=True, stop=True)
                            mm.then_inc(m_full, 1)
                        elif what == "route" and h == 2:
                            pe.wait_ge(r_counts, r + 1)
                            pe.matmul(ps_m[:, 0:E * TPB], before_b[:], both[:], start=True, stop=True)
                            pe.matmul(ps_m[:, E * TPB:2 * E * TPB], ones_b[:], both[:], start=True, stop=True).then_inc(m_full, 1)

                def act_body(act, b, part, pb, pn):
                    at, _, _ = numbers(part)
                    full, _ = bases(part, b)
                    n, r = b + 1, b - 1
                    for s in order(part):
                        what, h = s
                        if what == "prep" and h == 0:
                            act.wait_ge(m_full, full + at[s][0] + 1)
                            act.copy(xT[:], ps_m[:]).then_inc(m_free, 1)
                        elif what == "prep" and (A or h in (QR, QR + KR)):
                            q = h <= QR
                            if q and h == (1 if A else QR):
                                for k in range(H):
                                    wait(act, q_stacked[k], 16 * QSTACK * n)
                            if not q:
                                wait(act, k_stacked, 16 * KSTACK * n)
                            if A:
                                act.wait_ge(m_full, full + at[s][0] + 1)
                                if q:
                                    act.copy(q_hi[:, h - 1, :], ps_m[:]).then_inc(hi_ready, 1)
                                else:
                                    act.copy(k_hi[0:KP, :], ps_m[0:KP, :]).then_inc(hi_ready, 1)
                            else:
                                act.wait_ge(rot_ready, 2 * n + (1 if q else 2))
                                act.copy(q_hi[:, 0, :] if q else k_hi[:], rot[:, 2, :]).then_inc(hi_ready, 1)
                        elif what == "v":
                            wait(act, y_full, H * (n - 1))
                            act.wait_ge(m_full, full + at[s][0] + 1)
                            act.copy(v[:, pn, :, 0:DV], ps_m[:, 0:TPB * G * DV].rearrange(
                                "p (c d) -> p c d", d=DV)).then_inc(v_ready, 1)
                        elif what == "exp":
                            slot = b * H + h
                            for i, cols in enumerate(BANK_COLS):
                                if i == 0:
                                    wait(act, y_full, slot - 1)
                                act.wait_ge(st_full, 3 * slot + i + 1)
                                act.activation(prob[:, h % 2, i * 512:i * 512 + cols], ps_st[i][:, 0:cols],
                                               ACT.Exp).then_inc(st_free, 1)
                        elif what == "pv":
                            slot = b * H + h
                            y0, o0 = ((h % 2) * YM, (h % 4) * DV) if A else (0, h * DV)
                            if h == 0 and part in (MID, LATE, END):
                                act.wait_ge(m_full, full + at[("fin", 0)][0] + 1)
                            act.wait_ge(y_full, slot + 1)
                            act.copy(yT[o0:o0 + DV, h // 4, :], ps_y[y0:y0 + DV, :])
                            act.copy(y_sum[o0:o0 + DV, h // 4, :], ps_y[y0 + DV:y0 + YM, :]).then_inc(y_free, 1)
                        elif what == "route" and h == 0:
                            act.wait_ge(m_full, full + at[s][0] + 1)
                            act.copy(xT[:], ps_m[:]).then_inc(m_free, 1)
                        elif what == "route" and h == 1:
                            act.wait_ge(r_shifted, r + 1)
                            act.activation(sc[:], a0[:], ACT.Exp).then_inc(r_scored, 1)

                def dve_body(dve, b, part, pb, pn):
                    at, _, _ = numbers(part)
                    full, _ = bases(part, b)
                    n, r = b + 1, b - 1
                    route_chain = {}

                    def normalise(s, out, tiles, done):
                        for t in range(TPB):
                            ins = dve.tensor_scalar(out(t), flat(x[:, bass.ds(tiles + t, 1), :]), s["mean"][:, t:t + 1],
                                                    s["rstd"][:, t:t + 1], ALU.subtract, ALU.mult)
                        ins.then_inc(done, 1)

                    def over_e(t):
                        return t.unsqueeze(1).to_broadcast([P, E, TPB])

                    def by_t(t):
                        return t.rearrange("p e t -> p t e")

                    for s in order(part):
                        what, h = s
                        if what == "stats":
                            m, pm = (n, pn) if h == 0 else (n + 1, pb)
                            if not A:
                                dve.wait_ge(part_in[pm], 16 * (m - pm) + 32)
                                for k in range(2):
                                    if k == 1:
                                        dve.wait_ge(part_step, 2 * m + 1)
                                    for t in range(TPB):
                                        tile = bass.ds(m * TPB + t, 1)
                                        ins = dve.scalar_tensor_tensor(
                                            out=flat(x[:, tile, :]), in0=parts[:, pm, k, t, :], scalar=flat(weight[:, k:k + 1, tile]),
                                            in1=flat(x[:, tile, :]), op0=ALU.mult, op1=ALU.add)
                                    ins.then_inc(part_step, 1)
                                dve.wait_ge(part_step, 2 * m + 2)
                                dve.sem_inc(ln_turn, 1)
                            if A and part == FIRST and h == 1:
                                dve.wait_ge(x_rest, 16)
                            do = chain(dve, ln_step, LN_LINKS * m)
                            norm_stats(dve, ln, m * TPB, do)
                        elif what == "norm":
                            m = n + h
                            if h == 1:
                                dve.wait_ge(m_full, full + at[("prep", 0)][0] + 1)
                            normalise(ln, lambda t: xn[:, t, :], m * TPB, xn_ready)
                        elif what == "prep" and h > 0:
                            q = h <= QR
                            src = ps_m[0:P if q else KP, :]
                            dve.wait_ge(m_full, full + at[s][0] + 1)
                            if A:
                                hi, lo = (q_hi[:, h - 1, :], q_lo[:, h - 1, :]) if q else (k_hi[0:KP, :], k_lo[0:KP, :])
                                dve.wait_ge(hi_ready, 3 * n + h)
                                dve.tensor_tensor(lo, src, hi.bitcast(F32), ALU.subtract).then_inc(m_free, 1)
                            elif h in (1, 3):
                                wait(dve, hi_ready, 2 * n + h // 2)
                                dve.tensor_tensor(rot[:, 0, :], src, cos[:], ALU.mult).then_inc(m_free, 1)
                            else:
                                dve.tensor_tensor(rot[:, 1, :], src, sin[:], ALU.mult).then_inc(m_free, 1)
                                dve.wait_ge(m_free, bases(part, b)[1] + at[s][1] + 1)
                                dve.tensor_tensor(rot[:, 2, :], rot[:, 0, :], rot[:, 1, :], ALU.add).then_inc(rot_ready, 1)
                                hi, lo = (q_hi[:, 0, :], q_lo[:, 0, :]) if q else (k_hi[:], k_lo[:])
                                dve.wait_ge(rot_ready, 2 * n + h // 2)
                                dve.wait_ge(hi_ready, 2 * n + h // 2)
                                dve.tensor_tensor(lo, rot[:, 2, :], hi.bitcast(F32), ALU.subtract).then_inc(lo_ready, 1)
                        elif what == "max":
                            slot = n * H + h
                            for qt, last in ((3, 1), (2, 2), (0, 2), (1, 3)):
                                bank, col = S_PLACE[qt]
                                dve.wait_ge(s_full, 3 * slot + last)
                                dve.tensor_reduce(mx[:, qt, h:h + 1], ps_s[bank][:, col:col + (qt + 1) * P], AX_X,
                                                  ALU.max).then_inc(s_free, 1)
                        elif what == "max_t":
                            dve.wait_ge(m_full, full + at[s][0] + 1)
                            if A:
                                wait(dve, max_in, 16 * n)
                            dve.tensor_scalar(neg_max[:, 0 if A else pn, :], ps_m[0:H, :], -1.0, None, ALU.mult).then_inc(max_ready, 1)
                        elif what == "scale":
                            m = b if A and h == 0 else r
                            dve.wait_ge(y_free, H * m + H // YC * (h + 1))
                            dve.reciprocal(y_sum[:, h, :], y_sum[:, h, :]).then_inc(recip, 1)
                            dve.wait_ge(recip, YC * m + h + 1)
                            dve.tensor_tensor(yT[:, h, :], yT[:, h, :], y_sum[:, h, :], ALU.mult).then_inc(y_ready, 1)
                        elif what == "fin":
                            dve.wait_ge(m_full, full + at[s][0] + 1)
                            tiles = x[:, bass.ds(r * TPB, TPB), :].rearrange("p t d -> p (t d)")
                            dve.tensor_tensor(tiles, tiles, ps_m[:], ALU.add).then_inc(m_free, 1)
                            dve.wait_ge(m_free, bases(part, b)[1] + at[s][1] + 1)
                            dve.sem_inc(ln_turn, 1)
                        elif what == "r_stats":
                            do = route_chain["do"] = chain(dve, r_step, (LN_LINKS + ROUTE_LINKS) * r)
                            norm_stats(dve, rn, r * TPB, do)
                        elif what == "r_norm":
                            dve.wait_ge(rows_free, r + 1)
                            for k in range(2):
                                dve.tensor_copy(rows[:, k, :, D].bitcast(I32), dest[:, k, bass.ds(r * TPB, TPB)])
                            normalise(rn, lambda t: rows[:, 0, t, 0:D], r * TPB, r_normed)
                        elif what == "route" and h == 1:
                            do = route_chain["do"]
                            dve.wait_ge(m_full, full + at[s][0] + 1)
                            lg = ps_m[:, 0:TPB * E].rearrange("p (t e) -> p t e", e=E)
                            do(dve.tensor_reduce(r0[:], lg, AX_X, ALU.max))
                            do(dve.tensor_tensor(a0[:], lg.rearrange("p t e -> p e t"), over_e(r0[:]), ALU.subtract))
                            dve.sem_inc(m_free, 1)
                            dve.sem_inc(r_shifted, 1)
                        elif what == "choose":
                            do = route_chain["do"]
                            if h == 0:
                                dve.wait_ge(r_scored, r + 1)
                                do(dve.tensor_reduce(r0[:], by_t(sc[:]), AX_X, ALU.add))
                                do(dve.reciprocal(r1[:], r0[:]))
                                do(dve.tensor_tensor(sc[:], sc[:], over_e(r1[:]), ALU.mult))
                            do(dve.tensor_reduce(top[h][:], by_t(sc[:]), AX_X, ALU.max))
                            do(dve.tensor_tensor(a0[:], sc[:], over_e(top[h][:]), ALU.is_equal))
                            do(dve.tensor_tensor(a0[:], a0[:], rank_rev[:], ALU.mult))
                            do(dve.tensor_reduce(r0[:], by_t(a0[:]), AX_X, ALU.max))
                            do(dve.tensor_tensor(hot[h][:], a0[:], over_e(r0[:]), ALU.is_equal))
                            if h == 0:
                                do(dve.scalar_tensor_tensor(out=sc[:], in0=hot[0][:], scalar=-2.0, in1=sc[:],
                                                            op0=ALU.mult, op1=ALU.add))
                            else:
                                dve.tensor_tensor(both[:].rearrange("p (e t) -> p e t", e=E), hot[0][:], hot[1][:],
                                                  ALU.add).then_inc(r_counts, 1)
                                do(dve.scalar_tensor_tensor(out=r0[:], in0=top[0][:], scalar=TOPK_EPS, in1=top[1][:],
                                                            op0=ALU.add, op1=ALU.add))
                                do(dve.reciprocal(r1[:], r0[:]))
                                for k in range(2):
                                    ins = dve.tensor_tensor(weight[:, k, bass.ds(r * TPB, TPB)], top[k][:], r1[:], ALU.mult)
                                do(ins)
                        elif what == "route" and h == 2:
                            do = route_chain["do"]
                            dve.wait_ge(m_full, full + at[s][0] + 1)
                            tot = ps_m[:, E * TPB:2 * E * TPB]
                            do(dve.tensor_tensor_scan(incl[:].rearrange("p e t -> p (e t)"), carry[:].rearrange("p e t -> p (e t)"),
                                                      tot, 0.0, ALU.mult, ALU.add))
                            do(dve.tensor_tensor(pos[:], incl[:], tot.rearrange("p (e t) -> p e t", e=E), ALU.subtract))
                            do(dve.tensor_tensor(pos[:], pos[:], ps_m[:, 0:E * TPB].rearrange("p (e t) -> p e t", e=E), ALU.add))
                            dve.sem_inc(m_free, 1)
                            do(dve.tensor_tensor(pos[:], pos[:], placed_to[:].unsqueeze(2).to_broadcast([P, E, TPB]), ALU.add))
                            dve.tensor_tensor(placed_to[:], placed_to[:], incl[:, :, TPB - 1], ALU.add)
                            dve.tensor_tensor(a0[:], hot[0][:], pos[:], ALU.mult)
                            do(dve.tensor_tensor(a1[:], hot[1][:], pos[:], ALU.mult))
                            dve.tensor_reduce(r0[:], by_t(a0[:]), AX_X, ALU.add)
                            do(dve.tensor_reduce(r1[:], by_t(a1[:]), AX_X, ALU.add))
                            dve.tensor_copy(at_row[:, 0, :], r0[:])
                            do(dve.tensor_copy(at_row[:, 1, :], r1[:]))
                            dve.sem_inc(r_placed, 1)
                            assert do.count[0] == LN_LINKS + ROUTE_LINKS, do.count[0] - LN_LINKS

                def pool_body(pool, b, part, pb, pn):
                    n, r = b + 1, b - 1
                    for s in order(part):
                        what, h = s
                        if what == "exp":
                            slot = b * H + h
                            pool.wait_ge(st_free, 3 * slot + 3)
                            pool.sem_inc(mask_turn, 1)
                            for c0, step in ((0, 512), (896, P)):
                                ends = prob[:, h % 2, c0:c0 + 2 * step].rearrange("p (a n) -> p a n", a=2)[:, :, 0:P]
                                ins = pool.affine_select(out=ends, in_=ends, compare_op=ALU.is_ge, fill=0.0, base=0,
                                                         pattern=[[0, 2], [1, P]], channel_multiplier=-1)
                            ins.then_inc(masked, 1)
                        elif A and s in RAW:
                            k = RAW.index(s)
                            pool.wait_ge(raw_in, 16 * (3 * n + k + 1))
                            pool.sem_inc(mask_turn, 1)
                            if k < 2:
                                cols = bass.ds(n * (2 * FF) + k * FF, FF)
                                raw, hi, lo = w_raw[:], w_hi[:, cols], w_lo[:, cols]
                            else:
                                down = w_down[:, bass.ds(n * (2 * FF), 2 * FF)].rearrange("p (c k d) -> p c k d", c=FC, k=2)
                                raw, hi, lo = w_raw[:].rearrange("p (c d) -> p c d", c=FC), down[:, :, 0, :], down[:, :, 1, :]
                            pool.tensor_copy(hi, raw).then_inc(raw_step, 1)
                            pool.wait_ge(raw_step, 3 * n + k + 1)
                            pool.sem_inc(mask_turn, 1)
                            pool.tensor_tensor(lo, raw, hi.bitcast(F32), ALU.subtract).then_inc(raw_split, 1)
                        elif what == "r_norm":
                            pool.wait_ge(r_normed, r + 1)
                            pool.sem_inc(r_turn, 1)
                            pool.tensor_copy(rows[:, 1, :, 0:D], rows[:, 0, :, 0:D]).then_inc(r_copied, 1)
                        elif what == "scatter":
                            if h == 0:
                                pool.wait_ge(r_copied, r + 1)
                                pool.wait_ge(r_placed, r + 1)
                                pool.sem_inc(r_turn, 1)
                            for k in range(2):
                                pool.indirect_dma_start(gathered, bass.IndirectOffsetOnAxis(ap=at_row[:, k, h:h + 1], axis=0),
                                                        rows[:, k, h, :], None).then_inc(rows_in, 16)
                        elif what == "free":
                            pool.wait_ge(rows_in, 16 * 2 * TPB * (r + 1))
                            pool.sem_inc(rows_free, 1)

                def sp_body(sp, b, part, pb, pn):
                    n = b + 1
                    full, free = bases(part, b)
                    at, _, _ = numbers(part)

                    def load_parts(m, p):
                        wait(sp, part_step, 2 * (m - 1))
                        sp.sem_inc(load_turn, 1)
                        src = by_token.rearrange("(k t p) d -> p k t d", k=2, p=P)
                        for k in range(2):
                            sp.dma_start(parts[:, p, k, :, :], src[:, k, bass.ds(m * TPB, TPB), :]).then_inc(part_in[p], 16)

                    if part == FIRST and not A:
                        sp.dma_start(cos[:], io["rope_cos"]).then_inc(rope_in, 16)
                        sp.dma_start(sin[:], io["rope_sin"]).then_inc(rope_in, 16)
                    for s in order(part):
                        what, h = s
                        if A and s in RAW:
                            k = RAW.index(s)
                            wait(sp, raw_split, 3 * n + k)
                            sp.sem_inc(load_turn, 1)
                            raw = io["w_ffn"][:, bass.ds(n, 1), bass.ts(k, FF)].rearrange("p e n -> p (e n)")
                            sp.dma_start(w_raw[:], raw).then_inc(raw_in, 16)
                        if what == "stats" and not A:
                            load_parts(*((n, pn) if h == 0 else (n + 1, pb)))
                        elif what == "stack":
                            if A:
                                sp.wait_ge(m_free, free + at[("prep", PREP - 1)][1] + 1)
                            else:
                                sp.wait_ge(lo_ready, 2 * (n + 1))
                            sp.sem_inc(load_turn, 1)
                            wait(sp, st_full, 3 * H * (n - 1))
                            sp.sem_inc(load_turn, 1)
                            wait(sp, s_full, 3 * H * (n - 1))
                            for g in range(G):
                                src = slice(g * DV, (g + 1) * DV)
                                kparts = (k_hi, k_hi, k_lo) if A else (k_hi, k_lo)
                                for j, half in enumerate(kparts):
                                    sp.dma_start(k_stack[j * DV:(j + 1) * DV, pn, g, :].bitcast(F32), half[src, :].bitcast(F32))\
                                      .then_inc(k_stacked, 16)
                            for h in range(H):
                                src = slice((h % 4) * DV, (h % 4 + 1) * DV)
                                blocks = ([(j, h, half, h // 4) for j, half in enumerate((q_hi, q_lo, q_hi))] if A else
                                          [(j, 2 * h + a, half, 0) for a, half in enumerate((q_hi, q_lo)) for j in range(2)])
                                for j, to, half, c in blocks:
                                    sp.dma_start(q_stack[j * DV:(j + 1) * DV, pn, to, :].bitcast(F32), half[src, c, :].bitcast(F32))\
                                      .then_inc(q_stacked[h], 16)

                        elif what == "max_t" and A:
                            sp.wait_ge(max_ready, n + 1)
                            sp.dma_start(q_stack[KS:KX, pn, :, :].bitcast(F32), neg_max[:, 0, :].bitcast(F32)).then_inc(max_in, 16)

                set_up = N("set_up")
                n_i, n_t, n_c, one = T("n_i", [1, 2, E], I32), T("n_t", [1, 2, E]), T("n_c", [1, 2, E]), T("one", [1, E])
                pad_row = T("pad_row", [1, E], I32)
                spare = prob[0:1, :, :].rearrange("p a n -> p (a n)")
                step_no, g0, g1 = (spare[:, k * STEPS * E:(k + 1) * STEPS * E].rearrange("p (s e) -> p s e", e=E)
                                   for k in range(3))
                s_e, s_c, s_v = (spare[:, (3 * E + k) * STEPS:(3 * E + k + 1) * STEPS] for k in range(3))
                step_in, pads_known, pads_in, links = N("step_in"), N("pads_known"), N("pads_in"), N("plan_step")

                with nc.Block() as block:
                    @block.tensor
                    def _(pe):
                        whole(pe, pe_body)

                    @block.scalar
                    def _(act):
                        whole(act, act_body)

                    @block.vector
                    def _(dve):
                        if A:
                            ones = prob[KS:KX, :, :].rearrange("p a n -> p (a n)")[:, 0:2 * G * SEQ]
                            dve.memset(ones, 1.0).then_inc(ones_set, 1)
                            dve.wait_ge(ones_set, 1)
                            dve.tensor_copy(k_stack[KS:KX, :, :, :].rearrange("p a g n -> p (a g n)"), ones)
                        dve.tensor_copy(placed_to[:], region[:]).then_inc(set_up, 1)
                        dve.wait_ge(set_up, 1)
                        if not A:
                            dve.wait_ge(rope_in, 32)
                        whole(dve, dve_body)
                        do = chain(dve, links, 0)
                        ends = placed_to[0:1, :]
                        dve.tensor_copy(pad_row[:], ends).then_inc(pads_known, 1)
                        dve.memset(one[:], 1.0)
                        do(dve.tensor_tensor(n_t[:, 0, :], ends, region[0:1, :], ALU.subtract))
                        do(dve.tensor_scalar(n_i[:, 0, :], n_t[:, 0, :], float(P - 1), None, ALU.add))
                        do(dve.tensor_scalar(n_i[:, 1, :], n_i[:, 0, :], 7, None, ALU.logical_shift_right))
                        do(dve.tensor_copy(n_t[:, 1, :], n_i[:, 1, :]))
                        do(dve.tensor_tensor_scan(n_c[:, 0, :], one[:], n_t[:, 1, :], 0.0, ALU.mult, ALU.add))
                        do(dve.tensor_tensor(n_c[:, 1, :], n_c[:, 0, :], n_t[:, 1, :], ALU.subtract))
                        dve.wait_ge(step_in, 16)
                        first_tile = n_c[:, 1, :].unsqueeze(1).to_broadcast([1, STEPS, E])
                        do(dve.tensor_tensor(g0, step_no, first_tile, ALU.is_ge))
                        do(dve.tensor_tensor(g1, g0, first_tile, ALU.mult))
                        do(dve.tensor_reduce(s_e, g0, AX_X, ALU.add))
                        do(dve.tensor_reduce(s_c, g1, AX_X, ALU.max))
                        do(dve.tensor_scalar(s_e, s_e, -1.0, None, ALU.add))
                        do(dve.tensor_tensor(s_c, step_no[:, :, 0], s_c, ALU.subtract))
                        do(dve.tensor_scalar(s_c, s_c, float(P), float(-DUMMY_ROW), ALU.mult, ALU.add))
                        do(dve.scalar_tensor_tensor(out=s_c, in0=s_e, scalar=float(REGION), in1=s_c,
                                                    op0=ALU.mult, op1=ALU.add))
                        do(dve.tensor_scalar(s_v, step_no[:, :, 0], n_c[:, 0, E - 1:E], None, ALU.is_lt))
                        do(dve.tensor_tensor(s_c, s_c, s_v, ALU.mult))
                        do(dve.tensor_scalar(step_row[:], s_c, float(DUMMY_ROW), None, ALU.add))
                        do(dve.tensor_scalar(step_w[:], s_e, float(2 * FF), None, ALU.mult))

                    @block.gpsimd
                    def _(pool):
                        pool.sem_inc(rows_free, 1)
                        whole(pool, pool_body)

                    @block.sync
                    def _(sp):
                        whole(sp, sp_body)
                        sp.wait_ge(y_full, H * BATCH)
                        sp.dma_start(step_no, io["step_no"].rearrange("p (s e) -> p s e", e=E)).then_inc(step_in, 16)
                        sp.dma_start(gathered[DUMMY_ROW:ROWS, :], pad[:]).then_inc(pads_in, 16)
                        sp.wait_ge(pads_known, 1)
                        for e in range(E):
                            r = sp.value_load(pad_row[0:1, e:e + 1], min_val=e * REGION, max_val=e * REGION + TOKENS)
                            sp.dma_start(gathered[bass.ds(r, P), :], pad[:]).then_inc(pads_in, 16)
                        sp.wait_ge(pads_in, 16 * (E + 1))

        def expert_steps(tag):
            def T(n, s, dt, where):
                return sb(f"{n}_{tag}", s, dt, on=where)

            def N(n):
                return sem(f"{n}_{tag}")

            RING = 4
            UNROLL = 8
            on = ExitStack()
            with on:
                xg = T("xg", [P, RING, XROW], F32, on)
                to_row = T("to_row", [P, RING], U32, on)
                y = T("y_out", [P, RING, D], F32, on)
                x_hi, x_lo = T("x_hi", [P, 2, P], F32R, on), T("x_lo", [P, 2, P], F32R, on)
                up, h = T("up", [P, 2, FF], F32, on), T("h", [P, 2, FF], F32, on)
                y_low = T("y_low", [P, D], F32, on)
                h_hi, h_lo = T("h_hi", [P, 2, FF], F32R, on), T("h_lo", [P, 2, FF], F32R, on)
                ps_x, ps_h, ps_y = psum(f"ex{tag}", on), psum(f"eh{tag}", on), psum(f"ey{tag}", on)
                ps_u = [psum(f"eu{k}{tag}", on) for k in range(2)]
                ps_g = [psum(f"eg{k}{tag}", on) for k in range(2)]
                x_in = [N(f"x_in{k}") for k in range(RING)]
                out_done = [N(f"out_done{k}") for k in range(RING)]
                xt_full, xh_done, xl_done, row_kept = N("xt_full"), N("xh_done"), N("xl_done"), N("row_kept")
                u_full, g_full, u_done, h_done = N("u_full"), N("g_full"), N("u_done"), N("h_done")
                ht_full, hh_done, hl_done = N("ht_full"), N("hh_done"), N("hl_done")
                y_full, y_low_done, y_done = N("y_full"), N("y_low_done"), N("y_done")

                FIRST, LAST = -1, STEPS + 2
                LOOP = (6, STEPS - 2)

                def whole(eng, part):
                    for t in range(FIRST, LOOP[0]):
                        part(eng, t, t % RING)
                    with eng.Fori(0, (LOOP[1] - LOOP[0]) // UNROLL) as i:
                        for u in range(UNROLL):
                            part(eng, i * UNROLL + (LOOP[0] + u), (LOOP[0] + u) % RING)
                    for t in range(LOOP[1], LAST):
                        part(eng, t, t % RING)

                def live(t, lag):
                    return not isinstance(t, int) or 0 <= t - lag < STEPS

                def sure(eng, s, value):
                    if not isinstance(value, int) or value > 0:
                        eng.wait_ge(s, value)

                def pe_part(pe, t, u):
                    if live(t, 0):
                        w = pe.value_load(step_w[0:1, bass.ds(t, 1)], min_val=0, max_val=(E - 1) * 2 * FF)
                    if live(t, 2):
                        wd = pe.value_load(step_w[0:1, bass.ds(t - 2, 1)], min_val=0, max_val=(E - 1) * 2 * FF)
                    if live(t, -1):
                        k = (u + 1) % RING
                        sure(pe, x_in[k], 16 * ((t + 1) // RING + 1) if isinstance(t, int) else 4 * (t + 1 - k) + 16)
                        sure(pe, xl_done, t + 1)
                        pe.transpose(ps_x[:, 0:P], xg[:, k, 0:D], ident[:]).then_inc(xt_full, 1)
                    if live(t, 1):
                        k = (u - 1) % 2
                        sure(pe, h_done, t)
                        sure(pe, hl_done, t - 1)
                        for c in range(FC):
                            mm = pe.transpose(ps_h[:, bass.ts(c, P)], h[:, k, bass.ts(c, P)], ident[:])
                        mm.then_inc(ht_full, 1)
                    if live(t, 0):
                        k = u % 2
                        w_g, w_u = bass.ds(w, FF), bass.ds(w + FF, FF)
                        sure(pe, xl_done, t + 1)
                        sure(pe, h_done, t - 1)
                        pe.matmul(ps_u[k][:], x_hi[:, k, :], w_hi[:, w_u], start=True, stop=False)
                        pe.matmul(ps_u[k][:], x_hi[:, k, :], w_lo[:, w_u], start=False, stop=False)
                        pe.matmul(ps_u[k][:], x_lo[:, k, :], w_hi[:, w_u], start=False, stop=True).then_inc(u_full, 1)
                        pe.matmul(ps_g[k][:], x_lo[:, k, :], w_hi[:, w_g], start=True, stop=False)
                        pe.matmul(ps_g[k][:], x_hi[:, k, :], w_hi[:, w_g], start=False, stop=False)
                        pe.matmul(ps_g[k][:], x_hi[:, k, :], w_lo[:, w_g], start=False, stop=True).then_inc(g_full, 1)
                    if live(t, 2):
                        k = u % 2
                        sure(pe, hl_done, t - 1)
                        sure(pe, y_done, t - 2)
                        for c in range(FC):
                            cols = bass.ts(c, P)
                            w_d = bass.ds(wd + c * 2 * D, 2 * D)
                            pe.matmul(ps_y[:, 0:2 * D], h_hi[:, k, cols], w_down[:, w_d], start=(c == 0), stop=False)
                            mm = pe.matmul(ps_y[:, 0:2 * D], h_lo[:, k, cols], w_down[:, w_d], start=False, stop=(c == FC - 1))
                        mm.then_inc(y_full, 1)

                def act_part(act, t, u):
                    if live(t, -1):
                        sure(act, xt_full, t + 2)
                        sure(act, g_full, t)
                        act.copy(x_hi[:, (u + 1) % 2, :], ps_x[:, 0:P]).then_inc(xh_done, 1)
                    if live(t, 1):
                        sure(act, ht_full, t)
                        act.copy(h_hi[:, (u - 1) % 2, :], ps_h[:]).then_inc(hh_done, 1)
                    if live(t, 0):
                        sure(act, u_full, t + 1)
                        act.copy(up[:, u % 2, :], ps_u[u % 2][:]).then_inc(u_done, 1)
                    if live(t, 2):
                        sure(act, y_done, t - 2)
                        sure(act, y_full, t - 1)
                        act.copy(y_low[:], ps_y[:, D:2 * D]).then_inc(y_low_done, 1)

                def dve_part(dve, t, u):
                    if live(t, -1):
                        k = (u + 1) % 2
                        sure(dve, xh_done, t + 2)
                        dve.tensor_tensor(x_lo[:, k, :], ps_x[:, 0:P], x_hi[:, k, :].bitcast(F32), ALU.subtract).then_inc(xl_done, 1)
                    if live(t, 1):
                        k = (u - 1) % 2
                        sure(dve, hh_done, t)
                        dve.tensor_tensor(h_lo[:, k, :], ps_h[:], h_hi[:, k, :].bitcast(F32), ALU.subtract).then_inc(hl_done, 1)
                    if live(t, 0):
                        k = u % 2
                        sure(dve, u_done, t + 1)
                        sure(dve, g_full, t + 1)
                        sure(dve, ht_full, t - 1)
                        dve.scalar_tensor_tensor(out=h[:, k, :], in0=ps_g[k][:], scalar=0.0, in1=up[:, k, :],
                                                 op0=ALU.max, op1=ALU.mult).then_inc(h_done, 1)
                        sure(dve, out_done[u], 16 * (t // RING) if isinstance(t, int) else 4 * (t - u))
                        dve.tensor_copy(to_row[:, u:u + 1], xg[:, u, D:D + 1].bitcast(U32)).then_inc(row_kept, 1)
                    if live(t, 2):
                        k = (u - 2) % RING
                        sure(dve, out_done[k], 16 * ((t - 2) // RING) if isinstance(t, int) else 4 * (t - 2 - k))
                        sure(dve, y_low_done, t - 1)
                        dve.tensor_tensor(y[:, k, :], ps_y[:, 0:D], y_low[:], ALU.add).then_inc(y_done, 1)

                def pool_part(pool, t, u):
                    if live(t, 2):
                        k = (u - 2) % RING
                        sure(pool, row_kept, t - 1)
                        sure(pool, y_done, t - 1)
                        pool.sem_inc(out_turn, 1)
                        pool.indirect_dma_start(by_token, bass.IndirectOffsetOnAxis(ap=to_row[:, k:k + 1], axis=0),
                                                y[:, k, :], None, bounds_check=2 * TOKENS - 1, oob_is_err=False)\
                            .then_inc(out_done[k], 16)

                def sp_part(sp, t, u):
                    if live(t, -2):
                        k = (u + 2) % RING
                        r = sp.value_load(step_row[0:1, bass.ds(t + 2, 1)], min_val=0, max_val=DUMMY_ROW)
                        sure(sp, row_kept, t - 1)
                        sp.dma_start(xg[:, k, :], gathered[bass.ds(r, P), :]).then_inc(x_in[k], 16)

                out_turn = N("out_turn")
                with nc.Block() as block:
                    @block.tensor
                    def _(pe):
                        whole(pe, pe_part)

                    @block.scalar
                    def _(act):
                        whole(act, act_part)

                    @block.vector
                    def _(dve):
                        whole(dve, dve_part)

                    @block.gpsimd
                    def _(pool):
                        whole(pool, pool_part)
                        for k in range(RING):
                            pool.wait_ge(out_done[k], 16 * (STEPS // RING))

                    @block.sync
                    def _(sp):
                        sp_part(sp, -2, -2 % RING)
                        whole(sp, sp_part)


        def combine_and_store():
            tag = "out"
            on = ExitStack()
            with on:
                parts = sb(f"parts_{tag}", [P, 2, 2, TPB, D], on=on)
                part_in = [sem(f"part_in{k}_{tag}") for k in range(2)]
                first, added, stored = sem(f"first_{tag}"), sem(f"added_{tag}"), sem(f"stored_{tag}")
                src = by_token.rearrange("(k t p) d -> p k t d", k=2, p=P)
                with nc.Block() as block:
                    @block.sync
                    def _(sp):
                        def pair(i):
                            for u in range(2):
                                b = i * 2 + u
                                if not isinstance(i, int):
                                    sp.wait_ge(added, b - 1)
                                for k in range(2):
                                    sp.dma_start(parts[:, u, k, :, :], src[:, k, bass.ds(b * TPB, TPB), :]).then_inc(part_in[u], 16)
                        pair(0)
                        with sp.Fori(1, BATCH // 2) as i:
                            pair(i)

                    @block.vector
                    def _(dve):
                        with dve.Fori(0, BATCH // 2) as i:
                            for u in range(2):
                                b = i * 2 + u
                                dve.wait_ge(part_in[u], 32 * i + 32)
                                for k in range(2):
                                    if k == 1:
                                        dve.wait_ge(first, b + 1)
                                    for t in range(TPB):
                                        tile = bass.ds(b * TPB + t, 1)
                                        ins = dve.scalar_tensor_tensor(
                                            out=flat(x[:, tile, :]), in0=parts[:, u, k, t, :], scalar=flat(weight[:, k:k + 1, tile]),
                                            in1=flat(x[:, tile, :]), op0=ALU.mult, op1=ALU.add)
                                    ins.then_inc(first if k == 0 else added, 1)

                    @block.scalar
                    def _(act):
                        out = io["out"].rearrange("b (t p) d -> p (b t) d", p=P)
                        with act.Fori(0, BATCH) as b:
                            act.wait_ge(added, b + 1)
                            tiles = bass.ds(b * TPB, TPB)
                            act.dma_start(out[:, tiles, :], x[:, tiles, :]).then_inc(stored, 16)
                        act.wait_ge(stored, 16 * BATCH)

        load()
        attention("a")
        expert_steps("1")
        attention("b")
        expert_steps("2")
        combine_and_store()


def kernel(L0_attn_a_x, L0_attn_a_wq, L0_attn_a_wk_down, L0_attn_a_wv_down, L0_attn_a_wk_up, L0_attn_a_wv_up,
           L0_attn_a_wo, L0_attn_b_wq, L0_attn_b_wk, L0_attn_b_wv, L0_attn_b_wo, L0_ffn_Wr, L0_ffn_Wg, L0_ffn_Wu,
           L0_ffn_Wd):
    import concourse.bacc as bacc
    from concourse.bass_utils import run_bass_kernel_spmd

    arrays = dict(make_constants())
    arrays["x"] = L0_attn_a_x
    arrays["a_wq_t"] = np.transpose(L0_attn_a_wq)
    arrays["a_wku_t"] = np.transpose(L0_attn_a_wk_up)
    arrays["a_wvu_t"] = np.transpose(L0_attn_a_wv_up)
    arrays["a_wo"] = L0_attn_a_wo
    arrays["a_wk"] = L0_attn_a_wk_down
    arrays["a_wv"] = L0_attn_a_wv_down
    pair = np.arange(DB // 2)
    rows = np.concatenate([h * DB + np.concatenate([2 * pair, 2 * pair + 1]) for h in range(HB)])
    swap = np.concatenate([h * DB + np.concatenate([2 * pair + 1, 2 * pair]) for h in range(HB)])
    for name, w in (("b_wq", L0_attn_b_wq), ("b_wk", L0_attn_b_wk)):
        wt = np.transpose(w)
        arrays[name] = np.concatenate([wt[:, rows], wt[:, swap]], axis=1)
    arrays["b_wv"] = np.transpose(L0_attn_b_wv)
    arrays["b_wo"] = np.transpose(L0_attn_b_wo)
    arrays["router"] = np.transpose(L0_ffn_Wr)
    down = np.transpose(np.reshape(L0_ffn_Wd, (E, D, FC, P)), (3, 0, 2, 1)).reshape(P, E, FF)
    arrays["w_ffn"] = np.concatenate([np.transpose(L0_ffn_Wg, (2, 0, 1)), np.transpose(L0_ffn_Wu, (2, 0, 1)), down],
                                     axis=2)
    arrays = {f"in_{k}": np.ascontiguousarray(a) for k, a in arrays.items()}

    nc = bacc.Bacc("TRN2", target_bir_lowering=False, num_devices=1)
    io = {k[3:]: nc.dram_tensor(k, a.shape, mybir.dt.from_np(a.dtype), kind="ExternalInput").ap()
          for k, a in arrays.items()}
    io["out"] = nc.dram_tensor("out", (BATCH, SEQ, D), F32, kind="ExternalOutput").ap()
    build(nc, io)
    r = run_bass_kernel_spmd(nc, [arrays], core_ids=[0])
    return r.results[0]["out"]
```

```python
from contextlib import ExitStack

import numpy as np

import concourse.bass as bass
from concourse import mybir

ALU = mybir.AluOpType
ACT = mybir.ActivationFunctionType
AX_X = mybir.AxisListType.X
F32 = mybir.dt.float32
F32R = mybir.dt.float32r
BF16 = mybir.dt.bfloat16
I32 = mybir.dt.int32
U32 = mybir.dt.uint32

P = 128
BATCH = 8
SEQ = 512
D = 128
TPB = SEQ // P
NT = BATCH * TPB
TOKENS = NT * P
LN_EPS = 1e-5
RSQRT_MAGIC = 0x5F3759DF

HA, GA, DA, HDA = 8, 2, 32, 128
HB, DB = 2, 64
ROPE_BASE = 10000.0

E, FF = 8, 512
FC = FF // P
REGION = TOKENS + P
DUMMY_ROW = E * REGION
ROWS = DUMMY_ROW + P
XROW = D + 1
STEPS = 2 * TOKENS // P + E
NOWHERE = 1 << 20
TOPK_EPS = float(np.finfo(np.float32).eps)
MASKED = -1e30

S_PLACE = [(1, 384), (2, 0), (1, 0), (0, 0)]
ST_PLACE = [(0, 0), (1, 0), (2, 0), (1, 384)]
P_START = [0, 512, 1024, 896]
BANK_COLS = [512, 512, 256]


def make_constants():
    c = {}
    c["ident"] = np.eye(P, dtype=np.float32)
    q, k = np.arange(P)[:, None], np.arange(P)[None, :]
    c["causal"] = np.where(k > q, np.float32(MASKED), np.float32(0)).astype(np.float32)
    c["before"] = (q < k).astype(np.float32)
    sel = np.zeros((HB, HB, P), np.float32)
    for h in range(HB):
        sel[h, h] = 1
    c["select"] = sel
    theta = np.exp((np.log(np.float32(ROPE_BASE)) * np.arange(DB // 2, dtype=np.float32)
                    / np.float32(DB)).astype(np.float64)).astype(np.float32)
    args = (theta[:, None] * np.arange(SEQ, dtype=np.float32)[None, :]).astype(np.float64)
    scale = DB ** -0.25
    c["rope_cos"] = np.tile(np.cos(args) * scale, (2 * HB, 1)).astype(np.float32)
    sin = np.sin(args) * scale
    c["rope_sin"] = np.tile(np.concatenate([-sin, sin]), (HB, 1)).astype(np.float32)
    c["rank_rev"] = np.tile(np.repeat(np.arange(E, 0, -1, dtype=np.float32), TPB), (P, 1))
    c["region"] = np.tile(np.arange(E, dtype=np.float32) * REGION, (P, 1))
    carry = np.ones((E, TPB), np.float32)
    carry[:, 0] = 0
    c["carry"] = np.tile(carry.reshape(1, -1), (P, 1))
    c["step_no"] = np.repeat(np.arange(STEPS, dtype=np.float32), E)[None, :]
    t, p = np.arange(NT)[None, None, :], np.arange(P)[:, None, None]
    c["dest"] = (np.arange(2)[None, :, None] * TOKENS + t * P + p).astype(np.uint32).view(np.int32)
    pad = np.zeros((P, XROW), np.float32)
    pad[:, D] = np.full(P, NOWHERE, np.uint32).view(np.float32)
    c["pad"] = pad
    return c


def flat(ap):
    return ap.rearrange("p a n -> p (a n)")


def wait(eng, s, value):
    if not isinstance(value, int) or value > 0:
        eng.wait_ge(s, value)


def chain(eng, s, base):
    n = [0]

    def link(ins):
        n[0] += 1
        ins.then_inc(s, 1)
        eng.wait_ge(s, base + n[0])

    link.count = n
    return link


def build(nc, io):
    ctx = ExitStack()

    def sb(name, shape, dt=F32, on=ctx):
        return on.enter_context(nc.sbuf_tensor("sb_" + name, shape, dt))

    def psum(name, on):
        return on.enter_context(nc.psum_tensor("ps_" + name, [P, 512], F32))

    def sem(name):
        return ctx.enter_context(nc.semaphore(name))

    with ctx:
        x = sb("x", [P, NT, D])
        w_hi, w_lo = sb("w_hi", [P, E * 2 * FF], F32R), sb("w_lo", [P, E * 2 * FF], F32R)
        w_down = sb("w_down", [P, E * 2 * FF], F32R)
        ident = sb("ident", [P, P])
        ident_b, causal_b = sb("ident_b", [P, P], BF16), sb("causal_b", [P, P], BF16)
        before_b, ones_b = sb("before_b", [P, P], BF16), sb("ones_b", [P, P], BF16)
        router = sb("router", [P, E])
        rank_rev, carry = sb("rank_rev", [P, E, TPB]), sb("carry", [P, E, TPB])
        region = sb("region", [P, E])
        placed_to = sb("placed_to", [P, E])
        pad = sb("pad", [P, XROW])
        dest = sb("dest", [P, 2, NT], I32)
        weight = sb("weight", [P, 2, NT])
        step_row, step_w = sb("step_row", [1, STEPS], I32), sb("step_w", [1, STEPS], I32)

        x_rest = sem("x_rest")
        gathered = nc.dram_tensor("gathered", (ROWS, XROW), F32, kind="Internal").ap()
        by_token = nc.dram_tensor("by_token", (2 * TOKENS, D), F32, kind="Internal").ap()

        def load():
            on = ExitStack()
            with on:
                causal, before = sb("causal", [P, P], on=on), sb("before", [P, P], on=on)
                loaded, converted = sem("loaded"), sem("converted")
                x_src = io["x"].rearrange("b (t p) d -> p (b t) d", p=P)
                loads = [(causal[:], io["causal"]), (before[:], io["before"]), (ident[:], io["ident"]),
                         (x[:, 0:TPB, :], x_src[:, 0:TPB, :]),
                         (router[:], io["router"]), (rank_rev[:], io["rank_rev"].rearrange("p (e t) -> p e t", e=E)),
                         (carry[:], io["carry"].rearrange("p (e t) -> p e t", e=E)), (region[:], io["region"]),
                         (pad[:], io["pad"]), (dest[:], io["dest"])]
                with nc.Block() as block:
                    @block.sync
                    def _(sp):
                        for dst, src in loads:
                            sp.dma_start(dst, src).then_inc(loaded, 16)
                        sp.dma_start(x[:, TPB:, :], x_src[:, TPB:, :]).then_inc(x_rest, 16)
                        sp.wait_ge(loaded, 16 * len(loads))

                    @block.vector
                    def _(dve):
                        dve.memset(ones_b[:], 1.0)
                        dve.wait_ge(loaded, 16 * len(loads))
                        dve.tensor_copy(ident_b[:], ident[:])
                        dve.tensor_copy(causal_b[:], causal[:])
                        dve.tensor_copy(before_b[:], before[:]).then_inc(converted, 1)
                        dve.wait_ge(converted, 1)

        LN_LINKS = 15

        def norm_stats(dve, s, groups, do):
            cols = slice(groups[0][0] * TPB, (groups[-1][0] + 1) * TPB)
            st, mean, i0, i1 = s["st"][:, cols, :], s["mean"][:, cols], s["i"][:, 0, cols], s["i"][:, 1, cols]
            v, d, y, u = (s["t"][:, k, cols] for k in range(4))
            for slot, first in groups:
                for k in range(TPB):
                    ins = dve.bn_stats(s["st"][:, slot * TPB + k, :], flat(x[:, bass.ds(first + k, 1), :]))
            do(ins)
            dve.tensor_tensor(mean, st[:, :, 1], st[:, :, 4], ALU.add)
            dve.tensor_tensor(d, st[:, :, 1], st[:, :, 4], ALU.subtract)
            do(dve.tensor_tensor(v, st[:, :, 2], st[:, :, 5], ALU.add))
            dve.tensor_scalar(mean, mean, 0.5, None, ALU.mult)
            dve.tensor_scalar(v, v, 1.0 / D, LN_EPS, ALU.mult, ALU.add)
            do(dve.scalar_tensor_tensor(out=u, in0=d, scalar=0.25, in1=d, op0=ALU.mult, op1=ALU.mult))
            do(dve.tensor_tensor(v, v, u, ALU.add))
            do(dve.tensor_scalar(i0, v.bitcast(I32), 1, None, ALU.logical_shift_right))
            do(dve.tensor_scalar(i1, i0, -1.0, float(RSQRT_MAGIC), ALU.mult, ALU.add))
            src = i1.bitcast(F32)
            for k in range(3):
                dst = s["rstd"][:, cols] if k == 2 else (y, d)[k]
                do(dve.scalar_tensor_tensor(out=u, in0=src, scalar=-0.5, in1=src, op0=ALU.mult, op1=ALU.mult))
                do(dve.tensor_tensor(u, u, v, ALU.mult))
                ins = dve.scalar_tensor_tensor(out=dst, in0=u, scalar=1.5, in1=src, op0=ALU.add, op1=ALU.mult)
                src = dst
                do(ins)

        def norm_scratch(T):
            W = 2 * TPB
            return dict(st=T("ln_st", [P, W, 6]), t=T("ln_t", [P, 4, W]), i=T("ln_i", [P, 2, W], I32),
                        mean=T("ln_mean", [P, W]), rstd=T("ln_rstd", [P, W]))

        def attention(kind):
            A = kind == "a"
            H, G, DV = (HA, GA, DA) if A else (HB, HB, DB)
            NS = 1 if A else 2
            KS = 3 * DV if A else P
            KX = KS + 1 if A else P
            YM = 2 * DV
            YC = H * DV // P
            KR = 1 if A else 2
            QR = 2
            KP = G * DV
            KSTACK = (3 if A else 2) * G
            QSTACK = 3 if A else 4
            PREP = 1 + QR + KR
            ROUTE_LINKS = 26

            def N(n):
                return sem(f"{n}_{kind}")

            on = ExitStack()
            with on:
                def T(n, s, dt=F32):
                    return sb(f"{n}_{kind}", s, dt, on=on)

                wq, wk, wv, wo = T("wq", [P, QR * P]), T("wk", [P, KR * KP]), T("wv", [P, G * DV]), T("wo", [P, YC * D])
                select = None if A else T("select", [H, H * P], F32R)
                v = T("v", [P, 2, TPB * G, 2 * DV])
                w_in, w_ps, w_done = N("w_in"), N("w_ps"), N("w_done")
                if A:
                    with ExitStack() as raws:
                        wq_t, wo_r = sb("wq_t", [P, HA, D], on=raws), sb("wo_r", [P, HA, D], on=raws)
                        wku, wvu = sb("wku", [P, DA], on=raws), sb("wvu", [P, DA], on=raws)
                        ps_wq, ps_wo = psum("wq", raws), psum("wo", raws)
                        loads = [(wq_t[:], io["a_wq_t"].rearrange("(h k) d -> k h d", k=P)), (wku[:], io["a_wku_t"]),
                                 (wvu[:], io["a_wvu_t"]), (wo_r[:], io["a_wo"].rearrange("(h k) d -> k h d", k=P)),
                                 (wk[:], io["a_wk"]), (wv[:], io["a_wv"])]
                        with nc.Block() as block:
                            @block.sync
                            def _(sp):
                                for dst, src in loads:
                                    sp.dma_start(dst, src).then_inc(w_in, 16)

                            @block.vector
                            def _(dve):
                                dve.memset(v[:], 1.0)
                                dve.wait_ge(w_ps, 1)
                                dve.tensor_scalar(wq[:], ps_wq[:, 0:QR * P], HDA ** -0.5, None, ALU.mult).then_inc(w_done, 1)
                                dve.tensor_copy(wo[:], ps_wo[:, 0:YC * D]).then_inc(w_done, 1)

                            @block.tensor
                            def _(pe):
                                pe.wait_ge(w_in, 16 * len(loads))
                                for h in range(HA):
                                    pe.matmul(ps_wq[:, bass.ts(h, DA)], wq_t[:, h, :], wku[:], start=True, stop=True)
                                for h in range(HA):
                                    j, c = h % 4, h // 4
                                    mm = pe.matmul(ps_wo[DA * j:DA * j + DA, bass.ts(c, D)], wvu[:], wo_r[:, h, :],
                                                   start=True, stop=True)
                                mm.then_inc(w_ps, 1)
                else:
                    sel_raw = T("sel_raw", [H, H * P])
                    loads = [(wq[:], io["b_wq"]), (wk[:], io["b_wk"]), (wv[:], io["b_wv"]), (wo[:], io["b_wo"]),
                             (sel_raw[:], io["select"].rearrange("k h p -> k (h p)"))]

                xn, xT = T("xn", [P, TPB, D]), T("xT", [P, SEQ])
                q_hi, q_lo = T("q_hi", [P, 2 if A else 1, SEQ], F32R), T("q_lo", [P, 2 if A else 1, SEQ], F32R)
                k_hi, k_lo = T("k_hi", [P, SEQ], F32R), T("k_lo", [P, SEQ], F32R)
                q_stack = T("q_stack", [P, 2, H * NS, SEQ], F32R)
                k_stack = T("k_stack", [P, 2, G, SEQ], F32R)
                prob = T("prob", [P, 2, 1280])
                mx = T("mx", [P, TPB, H])
                neg_max = T("neg_max", [H, 1 if A else 2, SEQ], F32R)
                y_sum, yT = T("y_sum", [P, YC, SEQ]), T("yT", [P, YC, SEQ])
                ln = norm_scratch(T)
                if A:
                    w_raw = T("w_raw", [P, FF])
                else:
                    cos, sin, rot = T("cos", [P, SEQ]), T("sin", [P, SEQ]), T("rot", [P, 3, SEQ])
                    parts = T("parts", [P, 2, 2, TPB, D])
                rows = T("rows", [P, 2, TPB, XROW])
                sc, a0, a1 = T("sc", [P, E, TPB]), T("a0", [P, E, TPB]), T("a1", [P, E, TPB])
                hot = [T(f"hot{k}", [P, E, TPB]) for k in range(2)]
                both = T("both", [P, E * TPB], BF16)
                incl, pos = T("incl", [P, E, TPB]), T("pos", [P, E, TPB])
                top = [T(f"top{k}", [P, TPB]) for k in range(2)]
                r0, r1 = T("r0", [P, TPB]), T("r1", [P, TPB])
                at_row = T("at_row", [P, 2, TPB], U32)

                ps_s = [psum(f"s{i}{kind}", on) for i in range(3)]
                ps_st = [psum(f"st{i}{kind}", on) for i in range(3)]
                ps_y, ps_m = psum(f"y{kind}", on), psum(f"m{kind}", on)

                xn_ready, ln_step, ln_turn = N("xn_ready"), N("ln_step"), N("ln_turn")
                m_full, m_free = N("m_full"), N("m_free")
                hi_ready, k_stacked = N("hi_ready"), N("k_stacked")
                v_ready, max_ready = N("v_ready"), N("max_ready")
                q_stacked = [N(f"q_stacked{h}") for h in range(H)]
                s_full, s_free = N("s_full"), N("s_free")
                st_full, st_free, masked = N("st_full"), N("st_free"), N("masked")
                y_full, y_free, recip, y_ready = N("y_full"), N("y_free"), N("recip"), N("y_ready")
                mask_turn, load_turn = N("mask_turn"), N("load_turn")
                if A:
                    max_in, ones_set = N("max_in"), N("ones_set")
                    raw_in, raw_step, raw_split = N("raw_in"), N("raw_step"), N("raw_split")
                else:
                    rot_ready, lo_ready, rope_in = N("rot_ready"), N("lo_ready"), N("rope_in")
                    part_in, part_step = [N("part_in0"), N("part_in1")], N("part_step")
                r_normed, r_step, r_shifted, r_scored = N("r_normed"), N("r_step"), N("r_shifted"), N("r_scored")
                r_counts, r_placed, r_copied, r_turn = N("r_counts"), N("r_placed"), N("r_copied"), N("r_turn")
                rows_in, rows_free = N("rows_in"), N("rows_free")

                FIRST, START, MID, LATE, END, AFTER = range(6)

                if A:
                    ORDER = (("stats", 0), ("norm", 0), ("scale", 1), ("prep", 0), ("exp", 0), ("prep", 1),
                             ("exp", 1), ("prep", 2), ("prep", 3), ("stack", 0), ("fin", 0), ("pv", 0), ("v", 0),
                             ("stats", 1), ("exp", 2), ("norm", 1), ("pv", 1), ("r_norm", 0), ("exp", 3), ("max", 0),
                             ("pv", 2), ("route", 0), ("exp", 4), ("route", 1), ("max", 1), ("choose", 0),
                             ("max", 2), ("pv", 3), ("choose", 1), ("exp", 5), ("pv", 4), ("max", 3), ("pv", 5),
                             ("exp", 6), ("exp", 7), ("route", 2), ("scatter", 0), ("max", 4), ("scale", 0),
                             ("max", 5), ("pv", 6), ("scatter", 1), ("max", 6), ("max", 7), ("pv", 7),
                             ("scatter", 2), ("scatter", 3), ("max_t", 0), ("free", 0))
                else:
                    ORDER = (("add", 0), ("stats", 0), ("norm", 0), ("prep", 0), ("exp", 0), ("scale", 0),
                             ("add", 1), ("prep", 1), ("prep", 2), ("fin", 0), ("exp", 1), ("prep", 3), ("prep", 4),
                             ("v", 0), ("stack", 0), ("pv", 0), ("stats", 1), ("r_norm", 0), ("pv", 1), ("norm", 1),
                             ("route", 0), ("route", 1), ("choose", 0), ("choose", 1), ("max", 0), ("route", 2),
                             ("max", 1), ("scatter", 0), ("scatter", 1), ("scatter", 2), ("scatter", 3), ("free", 0),
                             ("max_t", 0))
                NEXT = ("prep", "stack", "v", "max", "max_t")
                NOW = ("exp", "pv")
                ROUTED = ("fin", "r_norm", "route", "choose", "scatter", "free")

                def order(part):
                    def takes_part(s):
                        what, h = s
                        if what == "stats":
                            return part == FIRST if h == 0 else True
                        if what in ("norm", "add"):
                            return part == FIRST if h == 0 else part <= MID
                        if what == "scale":
                            return part >= MID if h == YC - 1 else START <= part <= END
                        return (part <= LATE if what in NEXT else START <= part <= END if what in NOW else part >= MID)
                    return [s for s in ORDER if takes_part(s)]

                RAW = (("prep", 0), ("stack", 0), ("max", 3))
                OWN = ("v", "max_t")
                IN_ROUND = ("prep", "v", "max_t", "fin", "route")

                def is_round(s):
                    return s[0] in IN_ROUND

                def bank_of(s):
                    return ps_y if s[0] == "prep" and s[1] in (2, 4) else ps_m

                def numbers(part):
                    n = f = 0
                    at = {}
                    for s in order(part):
                        if is_round(s):
                            at[s] = (n, f)
                            n += 1
                            f += s[0] not in OWN
                    return at, n, f

                TOTALS = [numbers(p)[1:] for p in range(6)]

                def bases(part, b):
                    out = []
                    for k in range(2):
                        c = [t[k] for t in TOTALS]
                        out.append({FIRST: 0, START: c[0], MID: c[0] + c[1] + c[2] * (b - 1),
                                    LATE: c[0] + c[1] + c[2] * (BATCH - 3), END: c[0] + c[1] + c[2] * (BATCH - 3) + c[3],
                                    AFTER: c[0] + c[1] + c[2] * (BATCH - 3) + c[3] + c[4]}[part])
                    return out

                def whole(eng, body):
                    body(eng, -1, FIRST, 1, 0)
                    body(eng, 0, START, 0, 1)
                    with eng.Fori(0, (BATCH - 4) // 2) as i:
                        for u in (1, 2):
                            body(eng, i * 2 + u, MID, u % 2, (u + 1) % 2)
                    for b, part in ((BATCH - 3, MID), (BATCH - 2, LATE), (BATCH - 1, END), (BATCH, AFTER)):
                        body(eng, b, part, b % 2, (b + 1) % 2)

                def pe_body(pe, b, part, pb, pn):
                    at, _, _ = numbers(part)
                    full, free = bases(part, b)
                    n, r = b + 1, b - 1
                    steps = order(part)
                    rounds = [s for s in steps if is_round(s)]

                    def open_round(s):
                        before = [t for t in rounds[:rounds.index(s)] if bank_of(t) is bank_of(s)]
                        if before and before[-1][0] == "v":
                            pe.wait_ge(v_ready, n + 1)
                        elif before and before[-1][0] == "max_t":
                            pe.wait_ge(max_ready, n + 1)
                        elif before:
                            pe.wait_ge(m_free, free + at[before[-1]][1] + 1)
                        elif bank_of(s) is ps_y:
                            wait(pe, y_free, H * b if part >= START else 0)
                        else:
                            if START <= part <= END:
                                pe.wait_ge(max_ready, b + 1)
                            wait(pe, m_free, free)

                    for s in steps:
                        what, h = s
                        g = h * G // H
                        if is_round(s):
                            open_round(s)
                        if what == "prep":
                            if h == 0:
                                if part == FIRST and not A:
                                    pe.wait_ge(w_in, 16 * len(loads))
                                pe.wait_ge(xn_ready, n + 1)
                                for t in range(TPB):
                                    mm = pe.transpose(ps_m[:, bass.ts(t, P)], xn[:, t, :], ident[:])
                            elif h <= QR:
                                mm = pe.matmul(bank_of(s)[:], wq[:, bass.ts(h - 1, P)], xT[:], start=True, stop=True)
                            else:
                                k = h - 1 - QR
                                mm = pe.matmul(bank_of(s)[0:KP, :], wk[:, k * KP:(k + 1) * KP], xT[:], start=True, stop=True)
                            mm.then_inc(m_full, 1)
                        elif what == "v":
                            for t in range(TPB):
                                mm = pe.matmul(ps_m[:, t * G * DV:(t + 1) * G * DV], xT[:, bass.ts(t, P)], wv[:],
                                               start=True, stop=True)
                            mm.then_inc(m_full, 1)
                        elif what == "max":
                            slot = n * H + h
                            pe.wait_ge(q_stacked[h], 16 * QSTACK * (n + 1))
                            if h == 0:
                                pe.wait_ge(k_stacked, 16 * KSTACK * (n + 1))
                            for qt, need in ((3, 1), (2, 3), (0, None), (1, 4)):
                                bank, col = S_PLACE[qt]
                                if need:
                                    wait(pe, s_free, 4 * (slot - 1) + need)
                                for a in range(NS):
                                    pe.matmul(ps_s[bank][:, col:col + (qt + 1) * P], q_stack[0:KS, pn, h * NS + a, bass.ts(qt, P)],
                                              k_stack[0:KS, pn, g, 0:(qt + 1) * P], start=(a == 0), stop=(a == NS - 1))
                                mm = pe.matmul(ps_s[bank][:, col + qt * P:col + (qt + 1) * P], ident_b[:], causal_b[:],
                                               start=False, stop=True, skip_group_check=True)
                                if qt != 2:
                                    mm.then_inc(s_full, 1)
                        elif what == "max_t":
                            pe.wait_ge(s_free, 4 * H * (n + 1))
                            for qt in range(TPB):
                                mm = pe.transpose(ps_m[0:H, bass.ts(qt, P)], mx[:, qt, :], ident[:])
                            mm.then_inc(m_full, 1)
                        elif what == "exp":
                            slot = b * H + h
                            if h == 0:
                                if A:
                                    pe.wait_ge(max_in, 16 * (b + 1))
                                else:
                                    pe.wait_ge(max_ready, b + 1)
                            for kt, bank_no in ((0, 1), (1, 2), (3, None), (2, 3)):
                                bank, col = ST_PLACE[kt]
                                if bank_no:
                                    wait(pe, st_free, 3 * (slot - 1) + bank_no)
                                dst = ps_st[bank][:, col:col + (TPB - kt) * P]
                                for a in range(NS):
                                    mm = pe.matmul(dst, k_stack[0:KX, pb, g, bass.ts(kt, P)],
                                                   q_stack[0:KX, pb, h * NS + a, kt * P:SEQ], start=(a == 0), stop=A)
                                if not A:
                                    mm = pe.matmul(dst, select[:, bass.ts(h, P)], neg_max[:, pb, kt * P:SEQ],
                                                   start=False, stop=True)
                                if kt != 1:
                                    mm.then_inc(st_full, 1)
                        elif what == "pv":
                            slot = b * H + h
                            pe.wait_ge(masked, slot + 1)
                            if h == 0 and part <= LATE:
                                pe.wait_ge(m_free, free + at[("prep", PREP - 1 if PREP % 2 else PREP - 2)][1] + 1)
                            if h == 0:
                                pe.wait_ge(v_ready, b + 1)
                            wait(pe, y_free, slot - 1 if A else slot)
                            y0 = (h % 2) * YM if A else 0
                            for kt in range(TPB):
                                mm = pe.matmul(ps_y[y0:y0 + YM, kt * P:SEQ], v[:, pb, kt * G + g, :],
                                               prob[:, h % 2, P_START[kt]:P_START[kt] + (TPB - kt) * P],
                                               start=(kt == 0), stop=(kt == TPB - 1), skip_group_check=True)
                            mm.then_inc(y_full, 1)
                        elif what == "fin":
                            pe.wait_ge(y_ready, YC * (r + 1))
                            for qt in range(TPB):
                                for c in range(YC):
                                    mm = pe.matmul(ps_m[:, bass.ts(qt, D)], yT[:, c, bass.ts(qt, P)],
                                                   wo[:, bass.ts(c, D)], start=(c == 0), stop=(c == YC - 1))
                            mm.then_inc(m_full, 1)
                        elif what == "route" and h == 0:
                            pe.wait_ge(r_normed, r + 1)
                            for t in range(TPB):
                                mm = pe.transpose(ps_m[:, bass.ts(t, P)], rows[:, 0, t, 0:D], ident[:])
                            mm.then_inc(m_full, 1)
                        elif what == "route" and h == 1:
                            for t in range(TPB):
                                mm = pe.matmul(ps_m[:, bass.ts(t, E)], xT[:, bass.ts(t, P)], router[:], start=True, stop=True)
                            mm.then_inc(m_full, 1)
                        elif what == "route" and h == 2:
                            pe.wait_ge(r_counts, r + 1)
                            pe.matmul(ps_m[:, 0:E * TPB], before_b[:], both[:], start=True, stop=True)
                            pe.matmul(ps_m[:, E * TPB:2 * E * TPB], ones_b[:], both[:], start=True, stop=True).then_inc(m_full, 1)

                def act_body(act, b, part, pb, pn):
                    at, _, _ = numbers(part)
                    full, _ = bases(part, b)
                    n, r = b + 1, b - 1
                    for s in order(part):
                        what, h = s
                        if what == "prep" and h == 0:
                            act.wait_ge(m_full, full + at[s][0] + 1)
                            act.copy(xT[:], ps_m[:]).then_inc(m_free, 1)
                        elif what == "prep" and (A or h in (QR, QR + KR)):
                            q = h <= QR
                            if q and h == (1 if A else QR):
                                for k in range(H):
                                    wait(act, q_stacked[k], 16 * QSTACK * n)
                            if not q:
                                wait(act, k_stacked, 16 * KSTACK * n)
                            if A:
                                act.wait_ge(m_full, full + at[s][0] + 1)
                                if q:
                                    act.copy(q_hi[:, h - 1, :], bank_of(s)[:]).then_inc(hi_ready, 1)
                                else:
                                    act.copy(k_hi[0:KP, :], bank_of(s)[0:KP, :]).then_inc(hi_ready, 1)
                            else:
                                act.wait_ge(rot_ready, 2 * n + (1 if q else 2))
                                act.copy(q_hi[:, 0, :] if q else k_hi[:], rot[:, 2, :]).then_inc(hi_ready, 1)
                        elif what == "v":
                            wait(act, y_full, H * (n - 1))
                            act.wait_ge(m_full, full + at[s][0] + 1)
                            act.copy(v[:, pn, :, 0:DV], ps_m[:, 0:TPB * G * DV].rearrange(
                                "p (c d) -> p c d", d=DV)).then_inc(v_ready, 1)
                        elif what == "exp":
                            slot = b * H + h
                            for i, cols in enumerate(BANK_COLS):
                                if i == 0:
                                    wait(act, y_full, slot - 1)
                                act.wait_ge(st_full, 3 * slot + i + 1)
                                act.activation(prob[:, h % 2, i * 512:i * 512 + cols], ps_st[i][:, 0:cols],
                                               ACT.Exp).then_inc(st_free, 1)
                        elif what == "pv":
                            slot = b * H + h
                            y0, o0 = ((h % 2) * YM, (h % 4) * DV) if A else (0, h * DV)
                            if h == 0 and part in (MID, LATE, END):
                                act.wait_ge(m_full, full + at[("fin", 0)][0] + 1)
                            act.wait_ge(y_full, slot + 1)
                            act.copy(yT[o0:o0 + DV, h // 4, :], ps_y[y0:y0 + DV, :])
                            act.copy(y_sum[o0:o0 + DV, h // 4, :], ps_y[y0 + DV:y0 + YM, :]).then_inc(y_free, 1)
                        elif what == "route" and h == 0:
                            act.wait_ge(m_full, full + at[s][0] + 1)
                            act.copy(xT[:], ps_m[:]).then_inc(m_free, 1)
                        elif what == "route" and h == 1:
                            act.wait_ge(r_shifted, r + 1)
                            act.activation(sc[:], a0[:], ACT.Exp).then_inc(r_scored, 1)

                def dve_body(dve, b, part, pb, pn):
                    at, _, _ = numbers(part)
                    full, _ = bases(part, b)
                    n, r = b + 1, b - 1
                    route_chain = {}

                    def normalise(slot, out, tiles, done):
                        for t in range(TPB):
                            col = slot * TPB + t
                            ins = dve.tensor_scalar(out(t), flat(x[:, bass.ds(tiles + t, 1), :]), ln["mean"][:, col:col + 1],
                                                    ln["rstd"][:, col:col + 1], ALU.subtract, ALU.mult)
                        ins.then_inc(done, 1)

                    def over_e(t):
                        return t.unsqueeze(1).to_broadcast([P, E, TPB])

                    def by_t(t):
                        return t.rearrange("p e t -> p t e")

                    for s in order(part):
                        what, h = s
                        if what == "add":
                            m, pm = (n, pn) if h == 0 else (n + 1, pb)
                            dve.wait_ge(part_in[pm], 16 * (m - pm) + 32)
                            for k in range(2):
                                if k == 1:
                                    dve.wait_ge(part_step, 2 * m + 1)
                                for t in range(TPB):
                                    tile = bass.ds(m * TPB + t, 1)
                                    ins = dve.scalar_tensor_tensor(
                                        out=flat(x[:, tile, :]), in0=parts[:, pm, k, t, :], scalar=flat(weight[:, k:k + 1, tile]),
                                        in1=flat(x[:, tile, :]), op0=ALU.mult, op1=ALU.add)
                                ins.then_inc(part_step, 1)
                        elif what == "stats":
                            m = n + h
                            if not A and part <= MID:
                                dve.wait_ge(part_step, 2 * m + 2)
                                dve.sem_inc(ln_turn, 1)
                            if A and part == FIRST and h == 1:
                                dve.wait_ge(x_rest, 16)
                            groups = [(0, m * TPB)] if part <= MID else []
                            groups += [(1, r * TPB)] if part >= MID else []
                            norm_stats(dve, ln, groups, chain(dve, ln_step, LN_LINKS * (b + 1 + h)))
                        elif what == "norm":
                            m = n + h
                            if h == 1:
                                dve.wait_ge(m_full, full + at[("prep", 0)][0] + 1)
                            normalise(0, lambda t: xn[:, t, :], m * TPB, xn_ready)
                        elif s == ("prep", 0) and part == FIRST:
                            if A:
                                ones = prob[KS:KX, :, :].rearrange("p a n -> p (a n)")[:, 0:2 * G * SEQ]
                                dve.memset(ones, 1.0).then_inc(ones_set, 1)
                                dve.wait_ge(ones_set, 1)
                                dve.tensor_copy(k_stack[KS:KX, :, :, :].rearrange("p a g n -> p (a g n)"), ones)
                            else:
                                dve.memset(v[:], 1.0)
                        elif what == "prep" and h > 0:
                            q = h <= QR
                            src = bank_of(s)[0:P if q else KP, :]
                            if not A and part == FIRST and h == 1:
                                dve.wait_ge(w_in, 16 * len(loads))
                                dve.tensor_copy(select[:], sel_raw[:]).then_inc(w_done, 1)
                                dve.wait_ge(rope_in, 32)
                            dve.wait_ge(m_full, full + at[s][0] + 1)
                            if A:
                                hi, lo = (q_hi[:, h - 1, :], q_lo[:, h - 1, :]) if q else (k_hi[0:KP, :], k_lo[0:KP, :])
                                dve.wait_ge(hi_ready, 3 * n + h)
                                dve.tensor_tensor(lo, src, hi.bitcast(F32), ALU.subtract).then_inc(m_free, 1)
                            elif h in (1, 3):
                                wait(dve, rot_ready, 2 * n + h // 2)
                                dve.tensor_tensor(rot[:, 0, :], src, cos[:], ALU.mult).then_inc(m_free, 1)
                            else:
                                dve.tensor_tensor(rot[:, 1, :], src, sin[:], ALU.mult).then_inc(m_free, 1)
                        elif what == "max":
                            slot = n * H + h
                            for qt, last in ((3, 1), (2, 2), (0, 2), (1, 3)):
                                bank, col = S_PLACE[qt]
                                dve.wait_ge(s_full, 3 * slot + last)
                                dve.tensor_reduce(mx[:, qt, h:h + 1], ps_s[bank][:, col:col + (qt + 1) * P], AX_X,
                                                  ALU.max).then_inc(s_free, 1)
                        elif what == "max_t":
                            dve.wait_ge(m_full, full + at[s][0] + 1)
                            if A:
                                wait(dve, max_in, 16 * n)
                            dve.tensor_scalar(neg_max[:, 0 if A else pn, :], ps_m[0:H, :], -1.0, None, ALU.mult).then_inc(max_ready, 1)
                        elif what == "scale":
                            m = b if A and h == 0 else r
                            dve.wait_ge(y_free, H * m + H // YC * (h + 1))
                            dve.reciprocal(y_sum[:, h, :], y_sum[:, h, :]).then_inc(recip, 1)
                            dve.wait_ge(recip, YC * m + h + 1)
                            dve.tensor_tensor(yT[:, h, :], yT[:, h, :], y_sum[:, h, :], ALU.mult).then_inc(y_ready, 1)
                        elif what == "fin":
                            dve.wait_ge(m_full, full + at[s][0] + 1)
                            tiles = x[:, bass.ds(r * TPB, TPB), :].rearrange("p t d -> p (t d)")
                            dve.tensor_tensor(tiles, tiles, ps_m[:], ALU.add).then_inc(m_free, 1)
                            dve.wait_ge(m_free, bases(part, b)[1] + at[s][1] + 1)
                            dve.sem_inc(ln_turn, 1)
                        elif what == "r_norm":
                            dve.wait_ge(rows_free, r + 1)
                            for k in range(2):
                                dve.tensor_copy(rows[:, k, :, D].bitcast(I32), dest[:, k, bass.ds(r * TPB, TPB)])
                            normalise(1, lambda t: rows[:, 0, t, 0:D], r * TPB, r_normed)
                        elif what == "route" and h == 1:
                            do = route_chain["do"] = chain(dve, r_step, ROUTE_LINKS * r)
                            dve.wait_ge(m_full, full + at[s][0] + 1)
                            lg = ps_m[:, 0:TPB * E].rearrange("p (t e) -> p t e", e=E)
                            do(dve.tensor_reduce(r0[:], lg, AX_X, ALU.max))
                            do(dve.tensor_tensor(a0[:], lg.rearrange("p t e -> p e t"), over_e(r0[:]), ALU.subtract))
                            dve.sem_inc(m_free, 1)
                            dve.sem_inc(r_shifted, 1)
                        elif what == "choose":
                            do = route_chain["do"]
                            if h == 0:
                                dve.wait_ge(r_scored, r + 1)
                                do(dve.tensor_reduce(r0[:], by_t(sc[:]), AX_X, ALU.add))
                                do(dve.reciprocal(r1[:], r0[:]))
                                do(dve.tensor_tensor(sc[:], sc[:], over_e(r1[:]), ALU.mult))
                            do(dve.tensor_reduce(top[h][:], by_t(sc[:]), AX_X, ALU.max))
                            do(dve.tensor_tensor(a0[:], sc[:], over_e(top[h][:]), ALU.is_equal))
                            do(dve.tensor_tensor(a0[:], a0[:], rank_rev[:], ALU.mult))
                            do(dve.tensor_reduce(r0[:], by_t(a0[:]), AX_X, ALU.max))
                            do(dve.tensor_tensor(hot[h][:], a0[:], over_e(r0[:]), ALU.is_equal))
                            if h == 0:
                                do(dve.scalar_tensor_tensor(out=sc[:], in0=hot[0][:], scalar=-2.0, in1=sc[:],
                                                            op0=ALU.mult, op1=ALU.add))
                            else:
                                dve.tensor_tensor(both[:].rearrange("p (e t) -> p e t", e=E), hot[0][:], hot[1][:],
                                                  ALU.add).then_inc(r_counts, 1)
                                do(dve.scalar_tensor_tensor(out=r0[:], in0=top[0][:], scalar=TOPK_EPS, in1=top[1][:],
                                                            op0=ALU.add, op1=ALU.add))
                                do(dve.reciprocal(r1[:], r0[:]))
                                for k in range(2):
                                    ins = dve.tensor_tensor(weight[:, k, bass.ds(r * TPB, TPB)], top[k][:], r1[:], ALU.mult)
                                do(ins)
                        elif what == "route" and h == 2:
                            do = route_chain["do"]
                            dve.wait_ge(m_full, full + at[s][0] + 1)
                            tot = ps_m[:, E * TPB:2 * E * TPB]
                            do(dve.tensor_tensor_scan(incl[:].rearrange("p e t -> p (e t)"), carry[:].rearrange("p e t -> p (e t)"),
                                                      tot, 0.0, ALU.mult, ALU.add))
                            do(dve.tensor_tensor(pos[:], incl[:], tot.rearrange("p (e t) -> p e t", e=E), ALU.subtract))
                            do(dve.tensor_tensor(pos[:], pos[:], ps_m[:, 0:E * TPB].rearrange("p (e t) -> p e t", e=E), ALU.add))
                            dve.sem_inc(m_free, 1)
                            do(dve.tensor_tensor(pos[:], pos[:], placed_to[:].unsqueeze(2).to_broadcast([P, E, TPB]), ALU.add))
                            dve.tensor_tensor(placed_to[:], placed_to[:], incl[:, :, TPB - 1], ALU.add)
                            dve.tensor_tensor(a0[:], hot[0][:], pos[:], ALU.mult)
                            do(dve.tensor_tensor(a1[:], hot[1][:], pos[:], ALU.mult))
                            dve.tensor_reduce(r0[:], by_t(a0[:]), AX_X, ALU.add)
                            do(dve.tensor_reduce(r1[:], by_t(a1[:]), AX_X, ALU.add))
                            dve.tensor_copy(at_row[:, 0, :], r0[:])
                            do(dve.tensor_copy(at_row[:, 1, :], r1[:]))
                            dve.sem_inc(r_placed, 1)
                            assert do.count[0] == ROUTE_LINKS

                def pool_body(pool, b, part, pb, pn):
                    n, r = b + 1, b - 1
                    at, _, _ = numbers(part)
                    for s in order(part):
                        what, h = s
                        if what == "exp":
                            slot = b * H + h
                            pool.wait_ge(st_free, 3 * slot + 3)
                            pool.sem_inc(mask_turn, 1)
                            for c0, step in ((0, 512), (896, P)):
                                ends = prob[:, h % 2, c0:c0 + 2 * step].rearrange("p (a n) -> p a n", a=2)[:, :, 0:P]
                                ins = pool.affine_select(out=ends, in_=ends, compare_op=ALU.is_ge, fill=0.0, base=0,
                                                         pattern=[[0, 2], [1, P]], channel_multiplier=-1)
                            ins.then_inc(masked, 1)
                        elif A and s in RAW:
                            k = RAW.index(s)
                            pool.wait_ge(raw_in, 16 * (3 * n + k + 1))
                            pool.sem_inc(mask_turn, 1)
                            if k < 2:
                                cols = bass.ds(n * (2 * FF) + k * FF, FF)
                                raw, hi, lo = w_raw[:], w_hi[:, cols], w_lo[:, cols]
                            else:
                                down = w_down[:, bass.ds(n * (2 * FF), 2 * FF)].rearrange("p (c k d) -> p c k d", c=FC, k=2)
                                raw, hi, lo = w_raw[:].rearrange("p (c d) -> p c d", c=FC), down[:, :, 0, :], down[:, :, 1, :]
                            pool.tensor_copy(hi, raw).then_inc(raw_step, 1)
                            pool.wait_ge(raw_step, 3 * n + k + 1)
                            pool.sem_inc(mask_turn, 1)
                            pool.tensor_tensor(lo, raw, hi.bitcast(F32), ALU.subtract).then_inc(raw_split, 1)
                        elif what == "prep" and not A and h in (QR, QR + KR):
                            q = h == QR
                            hi, lo = (q_hi[:, 0, :], q_lo[:, 0, :]) if q else (k_hi[:], k_lo[:])
                            wait(pool, q_stacked[H - 1], 16 * QSTACK * n)
                            pool.sem_inc(mask_turn, 1)
                            wait(pool, lo_ready, 2 * n + h // 2 - 1)
                            pool.sem_inc(mask_turn, 1)
                            pool.wait_ge(m_free, bases(part, b)[1] + at[s][1] + 1)
                            pool.sem_inc(mask_turn, 1)
                            pool.tensor_tensor(rot[:, 2, :], rot[:, 0, :], rot[:, 1, :], ALU.add).then_inc(rot_ready, 1)
                            pool.wait_ge(hi_ready, 2 * n + h // 2)
                            pool.sem_inc(mask_turn, 1)
                            pool.tensor_tensor(lo, rot[:, 2, :], hi.bitcast(F32), ALU.subtract).then_inc(lo_ready, 1)
                        elif what == "r_norm":
                            pool.wait_ge(r_normed, r + 1)
                            pool.sem_inc(r_turn, 1)
                            pool.tensor_copy(rows[:, 1, :, 0:D], rows[:, 0, :, 0:D]).then_inc(r_copied, 1)
                        elif what == "scatter":
                            if h == 0:
                                pool.wait_ge(r_copied, r + 1)
                                pool.wait_ge(r_placed, r + 1)
                                pool.sem_inc(r_turn, 1)
                            for k in range(2):
                                pool.indirect_dma_start(gathered, bass.IndirectOffsetOnAxis(ap=at_row[:, k, h:h + 1], axis=0),
                                                        rows[:, k, h, :], None).then_inc(rows_in, 16)
                        elif what == "free":
                            pool.wait_ge(rows_in, 16 * 2 * TPB * (r + 1))
                            pool.sem_inc(rows_free, 1)

                def sp_body(sp, b, part, pb, pn):
                    n = b + 1
                    full, free = bases(part, b)
                    at, _, _ = numbers(part)

                    def load_parts(m, p):
                        wait(sp, part_step, 2 * (m - 1))
                        sp.sem_inc(load_turn, 1)
                        src = by_token.rearrange("(k t p) d -> p k t d", k=2, p=P)
                        for k in range(2):
                            sp.dma_start(parts[:, p, k, :, :], src[:, k, bass.ds(m * TPB, TPB), :]).then_inc(part_in[p], 16)

                    for s in order(part):
                        what, h = s
                        if A and s in RAW:
                            k = RAW.index(s)
                            wait(sp, raw_split, 3 * n + k)
                            sp.sem_inc(load_turn, 1)
                            raw = io["w_ffn"][:, bass.ds(n, 1), bass.ts(k, FF)].rearrange("p e n -> p (e n)")
                            sp.dma_start(w_raw[:], raw).then_inc(raw_in, 16)
                        if not A and s == ("stats", 0):
                            load_parts(n, pn)
                            for dst, src in loads:
                                sp.dma_start(dst, src).then_inc(w_in, 16)
                            sp.dma_start(cos[:], io["rope_cos"]).then_inc(rope_in, 16)
                            sp.dma_start(sin[:], io["rope_sin"]).then_inc(rope_in, 16)
                        elif not A and s == ("prep", 0) and part <= MID:
                            load_parts(n + 1, pb)
                        elif what == "stack":
                            if A:
                                sp.wait_ge(m_free, free + at[("prep", PREP - 1)][1] + 1)
                            else:
                                sp.wait_ge(lo_ready, 2 * (n + 1))
                            sp.sem_inc(load_turn, 1)
                            wait(sp, st_full, 3 * H * (n - 1))
                            sp.sem_inc(load_turn, 1)
                            wait(sp, s_full, 3 * H * (n - 1))
                            for g in range(G):
                                src = slice(g * DV, (g + 1) * DV)
                                kparts = (k_hi, k_hi, k_lo) if A else (k_hi, k_lo)
                                for j, half in enumerate(kparts):
                                    sp.dma_start(k_stack[j * DV:(j + 1) * DV, pn, g, :].bitcast(F32), half[src, :].bitcast(F32))\
                                      .then_inc(k_stacked, 16)
                            for h in range(H):
                                src = slice((h % 4) * DV, (h % 4 + 1) * DV)
                                blocks = ([(j, h, half, h // 4) for j, half in enumerate((q_hi, q_lo, q_hi))] if A else
                                          [(j, 2 * h + a, half, 0) for a, half in enumerate((q_hi, q_lo)) for j in range(2)])
                                for j, to, half, c in blocks:
                                    sp.dma_start(q_stack[j * DV:(j + 1) * DV, pn, to, :].bitcast(F32), half[src, c, :].bitcast(F32))\
                                      .then_inc(q_stacked[h], 16)

                        elif what == "max_t" and A:
                            sp.wait_ge(max_ready, n + 1)
                            sp.dma_start(q_stack[KS:KX, pn, :, :].bitcast(F32), neg_max[:, 0, :].bitcast(F32)).then_inc(max_in, 16)

                set_up = N("set_up")
                n_i, n_t, n_c, one = T("n_i", [1, 2, E], I32), T("n_t", [1, 2, E]), T("n_c", [1, 2, E]), T("one", [1, E])
                pad_row = T("pad_row", [1, E], I32)
                spare = prob[0:1, :, :].rearrange("p a n -> p (a n)")
                step_no, g0, g1 = (spare[:, k * STEPS * E:(k + 1) * STEPS * E].rearrange("p (s e) -> p s e", e=E)
                                   for k in range(3))
                s_e, s_c, s_v = (spare[:, (3 * E + k) * STEPS:(3 * E + k + 1) * STEPS] for k in range(3))
                step_in, pads_known, pads_in, links = N("step_in"), N("pads_known"), N("pads_in"), N("plan_step")

                with nc.Block() as block:
                    @block.tensor
                    def _(pe):
                        whole(pe, pe_body)

                    @block.scalar
                    def _(act):
                        whole(act, act_body)

                    @block.vector
                    def _(dve):
                        dve.tensor_copy(placed_to[:], region[:]).then_inc(set_up, 1)
                        dve.wait_ge(set_up, 1)
                        whole(dve, dve_body)
                        do = chain(dve, links, 0)
                        ends = placed_to[0:1, :]
                        dve.tensor_copy(pad_row[:], ends).then_inc(pads_known, 1)
                        dve.memset(one[:], 1.0)
                        do(dve.tensor_tensor(n_t[:, 0, :], ends, region[0:1, :], ALU.subtract))
                        do(dve.tensor_scalar(n_i[:, 0, :], n_t[:, 0, :], float(P - 1), None, ALU.add))
                        do(dve.tensor_scalar(n_i[:, 1, :], n_i[:, 0, :], 7, None, ALU.logical_shift_right))
                        do(dve.tensor_copy(n_t[:, 1, :], n_i[:, 1, :]))
                        do(dve.tensor_tensor_scan(n_c[:, 0, :], one[:], n_t[:, 1, :], 0.0, ALU.mult, ALU.add))
                        do(dve.tensor_tensor(n_c[:, 1, :], n_c[:, 0, :], n_t[:, 1, :], ALU.subtract))
                        dve.wait_ge(step_in, 16)
                        first_tile = n_c[:, 1, :].unsqueeze(1).to_broadcast([1, STEPS, E])
                        do(dve.tensor_tensor(g0, step_no, first_tile, ALU.is_ge))
                        do(dve.tensor_tensor(g1, g0, first_tile, ALU.mult))
                        do(dve.tensor_reduce(s_e, g0, AX_X, ALU.add))
                        do(dve.tensor_reduce(s_c, g1, AX_X, ALU.max))
                        do(dve.tensor_scalar(s_e, s_e, -1.0, None, ALU.add))
                        do(dve.tensor_tensor(s_c, step_no[:, :, 0], s_c, ALU.subtract))
                        do(dve.tensor_scalar(s_c, s_c, float(P), float(-DUMMY_ROW), ALU.mult, ALU.add))
                        do(dve.scalar_tensor_tensor(out=s_c, in0=s_e, scalar=float(REGION), in1=s_c,
                                                    op0=ALU.mult, op1=ALU.add))
                        do(dve.tensor_scalar(s_v, step_no[:, :, 0], n_c[:, 0, E - 1:E], None, ALU.is_lt))
                        do(dve.tensor_tensor(s_c, s_c, s_v, ALU.mult))
                        do(dve.tensor_scalar(step_row[:], s_c, float(DUMMY_ROW), None, ALU.add))
                        do(dve.tensor_scalar(step_w[:], s_e, float(2 * FF), None, ALU.mult))

                    @block.gpsimd
                    def _(pool):
                        pool.sem_inc(rows_free, 1)
                        whole(pool, pool_body)

                    @block.sync
                    def _(sp):
                        whole(sp, sp_body)
                        sp.wait_ge(y_full, H * BATCH)
                        sp.dma_start(step_no, io["step_no"].rearrange("p (s e) -> p s e", e=E)).then_inc(step_in, 16)
                        sp.dma_start(gathered[DUMMY_ROW:ROWS, :], pad[:]).then_inc(pads_in, 16)
                        sp.wait_ge(pads_known, 1)
                        for e in range(E):
                            r = sp.value_load(pad_row[0:1, e:e + 1], min_val=e * REGION, max_val=e * REGION + TOKENS)
                            sp.dma_start(gathered[bass.ds(r, P), :], pad[:]).then_inc(pads_in, 16)
                        sp.wait_ge(pads_in, 16 * (E + 1))

        def expert_steps(tag):
            def T(n, s, dt, where):
                return sb(f"{n}_{tag}", s, dt, on=where)

            def N(n):
                return sem(f"{n}_{tag}")

            RING = 4
            UNROLL = 8
            on = ExitStack()
            with on:
                xg = T("xg", [P, RING, XROW], F32, on)
                to_row = T("to_row", [P, RING], U32, on)
                y = T("y_out", [P, RING, D], F32, on)
                x_hi, x_lo = T("x_hi", [P, 2, P], F32R, on), T("x_lo", [P, 2, P], F32R, on)
                up, h = T("up", [P, 2, FF], F32, on), T("h", [P, 2, FF], F32, on)
                y_low = T("y_low", [P, D], F32, on)
                h_hi, h_lo = T("h_hi", [P, 2, FF], F32R, on), T("h_lo", [P, 2, FF], F32R, on)
                ps_x, ps_h, ps_y = psum(f"ex{tag}", on), psum(f"eh{tag}", on), psum(f"ey{tag}", on)
                ps_u = [psum(f"eu{k}{tag}", on) for k in range(2)]
                ps_g = [psum(f"eg{k}{tag}", on) for k in range(2)]
                x_in = [N(f"x_in{k}") for k in range(RING)]
                out_done = [N(f"out_done{k}") for k in range(RING)]
                xt_full, xh_done, xl_done, row_kept = N("xt_full"), N("xh_done"), N("xl_done"), N("row_kept")
                u_full, g_full, u_done, h_done = N("u_full"), N("g_full"), N("u_done"), N("h_done")
                ht_full, hh_done, hl_done = N("ht_full"), N("hh_done"), N("hl_done")
                y_full, y_low_done, y_done = N("y_full"), N("y_low_done"), N("y_done")

                FIRST, LAST = -1, STEPS + 2
                LOOP = (6, STEPS - 2)

                at_weights = []

                def whole(eng, part):
                    for t in range(FIRST, LOOP[0]):
                        part(eng, t, t % RING)
                    with eng.Fori(0, (LOOP[1] - LOOP[0]) // UNROLL) as i:
                        at_weights.clear()
                        for u in range(UNROLL):
                            part(eng, i * UNROLL + (LOOP[0] + u), (LOOP[0] + u) % RING)
                    at_weights.clear()
                    for t in range(LOOP[1], LAST):
                        part(eng, t, t % RING)

                def live(t, lag):
                    return not isinstance(t, int) or 0 <= t - lag < STEPS

                def pe_part(pe, t, u):
                    def load_at(step):
                        return pe.value_load(step_w[0:1, bass.ds(step, 1)], min_val=0, max_val=(E - 1) * 2 * FF)

                    w = load_at(t) if live(t, 0) else None
                    at_weights.append(w)
                    if live(t, 2):
                        wd = at_weights[-3] if len(at_weights) > 2 else load_at(t - 2)
                    if live(t, -1):
                        k = (u + 1) % RING
                        wait(pe, x_in[k], 16 * ((t + 1) // RING + 1) if isinstance(t, int) else 4 * (t + 1 - k) + 16)
                        wait(pe, xl_done, t + 1)
                        pe.transpose(ps_x[:, 0:P], xg[:, k, 0:D], ident[:]).then_inc(xt_full, 1)
                    if live(t, 1):
                        k = (u - 1) % 2
                        wait(pe, h_done, t)
                        wait(pe, hl_done, t - 1)
                        for c in range(FC):
                            mm = pe.transpose(ps_h[:, bass.ts(c, P)], h[:, k, bass.ts(c, P)], ident[:])
                        mm.then_inc(ht_full, 1)
                    if live(t, 0):
                        k = u % 2
                        w_g, w_u = bass.ds(w, FF), bass.ds(w + FF, FF)
                        wait(pe, xl_done, t + 1)
                        wait(pe, h_done, t - 1)
                        pe.matmul(ps_u[k][:], x_hi[:, k, :], w_hi[:, w_u], start=True, stop=False)
                        pe.matmul(ps_u[k][:], x_hi[:, k, :], w_lo[:, w_u], start=False, stop=False)
                        pe.matmul(ps_u[k][:], x_lo[:, k, :], w_hi[:, w_u], start=False, stop=True).then_inc(u_full, 1)
                        pe.matmul(ps_g[k][:], x_lo[:, k, :], w_hi[:, w_g], start=True, stop=False)
                        pe.matmul(ps_g[k][:], x_hi[:, k, :], w_hi[:, w_g], start=False, stop=False)
                        pe.matmul(ps_g[k][:], x_hi[:, k, :], w_lo[:, w_g], start=False, stop=True).then_inc(g_full, 1)
                    if live(t, 2):
                        k = u % 2
                        wait(pe, hl_done, t - 1)
                        wait(pe, y_done, t - 2)
                        for c in range(FC):
                            cols = bass.ts(c, P)
                            w_d = bass.ds(wd + c * 2 * D, 2 * D)
                            pe.matmul(ps_y[:, 0:2 * D], h_hi[:, k, cols], w_down[:, w_d], start=(c == 0), stop=False)
                            mm = pe.matmul(ps_y[:, 0:2 * D], h_lo[:, k, cols], w_down[:, w_d], start=False, stop=(c == FC - 1))
                        mm.then_inc(y_full, 1)

                def act_part(act, t, u):
                    if live(t, -1):
                        wait(act, xt_full, t + 2)
                        wait(act, g_full, t)
                        act.copy(x_hi[:, (u + 1) % 2, :], ps_x[:, 0:P]).then_inc(xh_done, 1)
                    if live(t, 1):
                        wait(act, ht_full, t)
                        act.copy(h_hi[:, (u - 1) % 2, :], ps_h[:]).then_inc(hh_done, 1)
                    if live(t, 0):
                        wait(act, u_full, t + 1)
                        act.copy(up[:, u % 2, :], ps_u[u % 2][:]).then_inc(u_done, 1)
                    if live(t, 2):
                        wait(act, y_done, t - 2)
                        wait(act, y_full, t - 1)
                        act.copy(y_low[:], ps_y[:, D:2 * D]).then_inc(y_low_done, 1)

                def dve_part(dve, t, u):
                    if live(t, -1):
                        k = (u + 1) % 2
                        wait(dve, xh_done, t + 2)
                        dve.tensor_tensor(x_lo[:, k, :], ps_x[:, 0:P], x_hi[:, k, :].bitcast(F32), ALU.subtract).then_inc(xl_done, 1)
                    if live(t, 1):
                        k = (u - 1) % 2
                        wait(dve, hh_done, t)
                        dve.tensor_tensor(h_lo[:, k, :], ps_h[:], h_hi[:, k, :].bitcast(F32), ALU.subtract).then_inc(hl_done, 1)
                    if live(t, 0):
                        k = u % 2
                        wait(dve, u_done, t + 1)
                        wait(dve, g_full, t + 1)
                        wait(dve, ht_full, t - 1)
                        dve.scalar_tensor_tensor(out=h[:, k, :], in0=ps_g[k][:], scalar=0.0, in1=up[:, k, :],
                                                 op0=ALU.max, op1=ALU.mult).then_inc(h_done, 1)
                        wait(dve, out_done[u], 16 * (t // RING) if isinstance(t, int) else 4 * (t - u))
                        dve.tensor_copy(to_row[:, u:u + 1], xg[:, u, D:D + 1].bitcast(U32)).then_inc(row_kept, 1)
                    if live(t, 2):
                        k = (u - 2) % RING
                        wait(dve, out_done[k], 16 * ((t - 2) // RING) if isinstance(t, int) else 4 * (t - 2 - k))
                        wait(dve, y_low_done, t - 1)
                        dve.tensor_tensor(y[:, k, :], ps_y[:, 0:D], y_low[:], ALU.add).then_inc(y_done, 1)

                def pool_part(pool, t, u):
                    if live(t, 2):
                        k = (u - 2) % RING
                        wait(pool, row_kept, t - 1)
                        wait(pool, y_done, t - 1)
                        pool.sem_inc(out_turn, 1)
                        pool.indirect_dma_start(by_token, bass.IndirectOffsetOnAxis(ap=to_row[:, k:k + 1], axis=0),
                                                y[:, k, :], None, bounds_check=2 * TOKENS - 1, oob_is_err=False)\
                            .then_inc(out_done[k], 16)

                def sp_part(sp, t, u):
                    if live(t, -2):
                        k = (u + 2) % RING
                        r = sp.value_load(step_row[0:1, bass.ds(t + 2, 1)], min_val=0, max_val=DUMMY_ROW)
                        wait(sp, row_kept, t - 1)
                        sp.dma_start(xg[:, k, :], gathered[bass.ds(r, P), :]).then_inc(x_in[k], 16)

                out_turn = N("out_turn")
                with nc.Block() as block:
                    @block.tensor
                    def _(pe):
                        whole(pe, pe_part)

                    @block.scalar
                    def _(act):
                        whole(act, act_part)

                    @block.vector
                    def _(dve):
                        whole(dve, dve_part)

                    @block.gpsimd
                    def _(pool):
                        whole(pool, pool_part)
                        for k in range(RING):
                            pool.wait_ge(out_done[k], 16 * (STEPS // RING))

                    @block.sync
                    def _(sp):
                        sp_part(sp, -2, -2 % RING)
                        whole(sp, sp_part)


        def combine_and_store():
            tag = "out"
            RING = 4
            on = ExitStack()
            with on:
                parts = sb(f"parts_{tag}", [P, RING, 2, TPB, D], on=on)
                part_in = [sem(f"part_in{k}_{tag}") for k in range(RING)]
                first, added, stored = sem(f"first_{tag}"), sem(f"added_{tag}"), sem(f"stored_{tag}")
                src = by_token.rearrange("(k t p) d -> p k t d", k=2, p=P)
                with nc.Block() as block:
                    @block.sync
                    def _(sp):
                        def group(i, reused):
                            for u in range(RING):
                                b = i * RING + u
                                if reused:
                                    sp.wait_ge(added, b + 1 - RING)
                                for k in range(2):
                                    sp.dma_start(parts[:, u, k, :, :], src[:, k, bass.ds(b * TPB, TPB), :]).then_inc(part_in[u], 16)
                        group(0, False)
                        with sp.Fori(1, BATCH // RING) as i:
                            group(i, True)

                    @block.vector
                    def _(dve):
                        with dve.Fori(0, BATCH // RING) as i:
                            for u in range(RING):
                                b = i * RING + u
                                dve.wait_ge(part_in[u], 32 * i + 32)
                                for k in range(2):
                                    if k == 1:
                                        dve.wait_ge(first, b + 1)
                                    for t in range(TPB):
                                        tile = bass.ds(b * TPB + t, 1)
                                        ins = dve.scalar_tensor_tensor(
                                            out=flat(x[:, tile, :]), in0=parts[:, u, k, t, :], scalar=flat(weight[:, k:k + 1, tile]),
                                            in1=flat(x[:, tile, :]), op0=ALU.mult, op1=ALU.add)
                                    ins.then_inc(first if k == 0 else added, 1)

                    @block.scalar
                    def _(act):
                        out = io["out"].rearrange("b (t p) d -> p (b t) d", p=P)
                        with act.Fori(0, BATCH) as b:
                            act.wait_ge(added, b + 1)
                            tiles = bass.ds(b * TPB, TPB)
                            act.dma_start(out[:, tiles, :], x[:, tiles, :]).then_inc(stored, 16)
                        act.wait_ge(stored, 16 * BATCH)

        load()
        attention("a")
        expert_steps("1")
        attention("b")
        expert_steps("2")
        combine_and_store()


def kernel(L0_attn_a_x, L0_attn_a_wq, L0_attn_a_wk_down, L0_attn_a_wv_down, L0_attn_a_wk_up, L0_attn_a_wv_up,
           L0_attn_a_wo, L0_attn_b_wq, L0_attn_b_wk, L0_attn_b_wv, L0_attn_b_wo, L0_ffn_Wr, L0_ffn_Wg, L0_ffn_Wu,
           L0_ffn_Wd):
    import concourse.bacc as bacc
    from concourse.bass_utils import run_bass_kernel_spmd

    arrays = dict(make_constants())
    arrays["x"] = L0_attn_a_x
    arrays["a_wq_t"] = np.transpose(L0_attn_a_wq)
    arrays["a_wku_t"] = np.transpose(L0_attn_a_wk_up)
    arrays["a_wvu_t"] = np.transpose(L0_attn_a_wv_up)
    arrays["a_wo"] = L0_attn_a_wo
    arrays["a_wk"] = L0_attn_a_wk_down
    arrays["a_wv"] = L0_attn_a_wv_down
    pair = np.arange(DB // 2)
    rows = np.concatenate([h * DB + np.concatenate([2 * pair, 2 * pair + 1]) for h in range(HB)])
    swap = np.concatenate([h * DB + np.concatenate([2 * pair + 1, 2 * pair]) for h in range(HB)])
    for name, w in (("b_wq", L0_attn_b_wq), ("b_wk", L0_attn_b_wk)):
        wt = np.transpose(w)
        arrays[name] = np.concatenate([wt[:, rows], wt[:, swap]], axis=1)
    arrays["b_wv"] = np.transpose(L0_attn_b_wv)
    arrays["b_wo"] = np.transpose(L0_attn_b_wo)
    arrays["router"] = np.transpose(L0_ffn_Wr)
    down = np.transpose(np.reshape(L0_ffn_Wd, (E, D, FC, P)), (3, 0, 2, 1)).reshape(P, E, FF)
    arrays["w_ffn"] = np.concatenate([np.transpose(L0_ffn_Wg, (2, 0, 1)), np.transpose(L0_ffn_Wu, (2, 0, 1)), down],
                                     axis=2)
    arrays = {f"in_{k}": np.ascontiguousarray(a) for k, a in arrays.items()}

    nc = bacc.Bacc("TRN2", target_bir_lowering=False, num_devices=1)
    io = {k[3:]: nc.dram_tensor(k, a.shape, mybir.dt.from_np(a.dtype), kind="ExternalInput").ap()
          for k, a in arrays.items()}
    io["out"] = nc.dram_tensor("out", (BATCH, SEQ, D), F32, kind="ExternalOutput").ap()
    build(nc, io)
    r = run_bass_kernel_spmd(nc, [arrays], core_ids=[0])
    return r.results[0]["out"]
```
